# Optimizing a Trainium2 kernel written in Bass

```python
import numpy as np
import jax
import jax.numpy as jnp

def _softmax(x, axis=-1):
    return jax.nn.softmax(x, axis=axis)

def _gelu(x):
    return jax.nn.gelu(x, approximate=True)

def _silu(x):
    return jax.nn.silu(x)

def _sigmoid(x):
    return jax.nn.sigmoid(x)

def _layernorm(x, axis=-1, eps=1e-05):
    m = jnp.mean(x, axis=axis, keepdims=True)
    v = jnp.var(x, axis=axis, keepdims=True)
    return (x - m) / jnp.sqrt(v + eps)

def _scatter_add(tgt, idx, src, axis=0):
    return tgt.at[idx].add(src)

def _segment_sum(src, seg, n):
    return jax.ops.segment_sum(src, seg, n)
kernel_name = 'mk_adj_resnorm_d2_adj_r2_045291'

def setup_inputs(seed: int=0):
    np.random.seed(seed)
    _w = jnp.asarray

    def _rec_inputs():
        import jax
        import jax.numpy as jnp
        _gk = jax.random.key(seed)
        x = -8.776e-05 + 1 * jax.random.normal(jax.random.fold_in(_gk, 1), (10000, 128), jnp.float32)
        _a = jax.random.bernoulli(jax.random.fold_in(_gk, 2), 0.0002, (10000, 10000))
        _a = jnp.logical_or(_a, jnp.eye(10000, dtype=bool))
        _af = _a.astype(jnp.float32)
        _af = _af * jax.random.uniform(jax.random.fold_in(_gk, 3), (10000, 10000), jnp.float32, 0.05, 1)
        adj = _af
        return (x, adj)
    x, adj = _rec_inputs()

    def _L0_gnn_setup():
        import jax, jax.numpy as jnp
        import numpy as np
        N_USER = 10000
        N_ITEM = 10000
        HID = 128
        key = jax.random.key(seed)
        k1, k2, k3, k4, k5, k6, k7 = jax.random.split(key, 7)
        scale = 1.0 / np.sqrt(HID)
        return {'user_feat': jax.random.normal(k1, (N_USER, HID), dtype=jnp.float32), 'item_feat': jax.random.normal(k2, (N_ITEM, HID), dtype=jnp.float32), 'adj': jax.random.uniform(k3, (N_USER, N_ITEM), dtype=jnp.float32), 'W_item': jax.random.uniform(k4, (HID, HID), dtype=jnp.float32, minval=-scale, maxval=scale), 'b_item': jax.random.uniform(k5, (HID,), dtype=jnp.float32, minval=-scale, maxval=scale), 'W_user': jax.random.uniform(k6, (HID, HID), dtype=jnp.float32, minval=-scale, maxval=scale), 'b_user': jax.random.uniform(k7, (HID,), dtype=jnp.float32, minval=-scale, maxval=scale)}
    _L0_gnn_all = _L0_gnn_setup()
    _L0_gnn_in = {k: v for k, v in _L0_gnn_all.items() if k in ('item_feat', 'W_item', 'b_item', 'W_user', 'b_user')}
    del _L0_gnn_all

    def _L1_gnn_setup():
        import jax, jax.numpy as jnp
        import numpy as np
        N = 4096
        F_IN = 128
        F_OUT = 128
        key = jax.random.key(seed)
        k1, k2, k3 = jax.random.split(key, 3)
        H = jax.random.normal(k1, (N, F_IN), dtype=jnp.float32)
        A_tilde = jax.random.uniform(k2, (N, N), dtype=jnp.float32)
        limit = np.sqrt(6.0 / (F_IN + F_OUT)).astype(np.float32)
        W = jax.random.uniform(k3, (F_IN, F_OUT), dtype=jnp.float32, minval=-limit, maxval=limit)
        return {'H': H, 'A_tilde': A_tilde, 'W': W}
    _L1_gnn_all = _L1_gnn_setup()
    _L1_gnn_in = {k: v for k, v in _L1_gnn_all.items() if k in ('W',)}
    del _L1_gnn_all
    return {'x': x, 'adj': adj, 'L0_gnn_item_feat': _L0_gnn_in['item_feat'], 'L0_gnn_W_item': _L0_gnn_in['W_item'], 'L0_gnn_b_item': _L0_gnn_in['b_item'], 'L0_gnn_W_user': _L0_gnn_in['W_user'], 'L0_gnn_b_user': _L0_gnn_in['b_user'], 'L1_gnn_W': _L1_gnn_in['W']}

def reference(x, adj, L0_gnn_item_feat, L0_gnn_W_item, L0_gnn_b_item, L0_gnn_W_user, L0_gnn_b_user, L1_gnn_W):
    import jax
    import jax.numpy as jnp

    def _L0_gnn_ref(user_feat, item_feat, adj, W_item, b_item, W_user, b_user):
        import jax, jax.numpy as jnp
        import numpy as np
        N_USER = 10000
        N_ITEM = 10000
        HID = 128
        h = item_feat @ W_item.T + b_item
        b = user_feat @ W_user.T + b_user
        return jax.nn.relu(adj @ h + b)

    def _L1_gnn_ref(H, A_tilde, W):
        import jax, jax.numpy as jnp
        import numpy as np
        N = 4096
        F_IN = 128
        F_OUT = 128
        d_inv_sqrt = jnp.sum(A_tilde, axis=1) ** (-0.5)
        A_norm = d_inv_sqrt[:, None] * A_tilde * d_inv_sqrt[None, :]
        H_next = A_norm @ H @ W
        return jax.nn.relu(H_next)
    x = _layernorm(x + _L0_gnn_ref(x, L0_gnn_item_feat, adj, L0_gnn_W_item, L0_gnn_b_item, L0_gnn_W_user, L0_gnn_b_user), axis=-1)
    x = _layernorm(x + _L1_gnn_ref(x, adj, L1_gnn_W), axis=-1)
    return x

_drawn_inputs = setup_inputs


def setup_inputs(seed=0):
    import zlib

    import numpy as np

    out = dict(_drawn_inputs(seed))
    spreads = {}
    factors = {}
    for name, (base, spread) in spreads.items():
        noise = np.random.default_rng([zlib.crc32(name.encode()), seed]).standard_normal(out[name].shape)
        drawn = base * np.exp(spread * noise) if base else spread * noise
        out[name] = jnp.asarray(drawn.astype(out[name].dtype))
    for name, factor in factors.items():
        out[name] = (out[name] * factor).astype(out[name].dtype)
    return out
```

```python
from contextlib import ExitStack

import concourse.bass as bass
from concourse import mybir

P = 128
F32 = mybir.dt.float32
ALU = mybir.AluOpType
ACT = mybir.ActivationFunctionType
EPS = 1e-5
GB = 4


def gnn_kernel(nc, x, adj, item, W_item, b_item, W_user, b_user, W1, out):
    N, D = x.shape
    assert D == P
    NT = -(-N // P)
    TAIL0 = N - P
    NFULL = N // P
    REST = N - NFULL * P
    PAIRS = (NT - 1) // 2
    assert NT == 2 * PAIRS + 1 and 0 < REST
    widths = [P] * NFULL + [REST]
    groups = [list(range(g, min(g + GB, NT))) for g in range(0, NT, GB)]
    NG = len(groups)
    assert NG % 2 == 0
    HG = NG // 2
    C = D + 1

    x1_dram = nc.dram_tensor("x1_scratch", (N, D), F32, kind="Internal").ap()
    y_dram = nc.dram_tensor("y_scratch", (N, D), F32, kind="Internal").ap()

    with ExitStack() as ctx:
        def sb(name, shape, dt=F32):
            return ctx.enter_context(nc.sbuf_tensor(name, shape, dt))

        def ps(name, shape, dt=F32):
            return ctx.enter_context(nc.psum_tensor(name, shape, dt))

        def sem(name):
            return ctx.enter_context(nc.semaphore(name))

        feat = sb("feat", [P, NT, C])
        adj_rows = [sb(f"adj_rows{b}", [P, N]) for b in range(2)]
        adjT = [sb(f"adjT{b}", [P, GB * P]) for b in range(2)]
        ident = sb("ident", [P, P])
        w_raw = sb("w_raw", [P, 2, D])
        WiT = sb("WiT", [P, D])
        WuT = sb("WuT", [P, D])
        W1sb = sb("W1sb", [P, D])
        b_rows = sb("b_rows", [1, 2, D])
        ones = sb("ones", [1, P])
        dinv = sb("dinv", [P, NT])
        xin = [sb(f"xin{b}", [P, D]) for b in range(2)]
        xT = sb("xT", [P, P])
        res = sb("res", [P, D])
        stats = sb("stats", [P, 6])
        mv = sb("mv", [P, 3])
        rs = sb("rs", [P, 2])
        sq = sb("sq", [P, 2])
        x1 = [sb(f"x1_{b}", [P, D]) for b in range(2)]
        y = [sb(f"y_{b}", [P, D]) for b in range(2)]
        zs = sb("zs", [P, D])

        psT = [ps(f"psT{b}", [P, GB * P]) for b in range(2)]
        psO = ps("psO", [P, 512])
        psX = ps("psX", [P, 512])
        psZ = ps("psZ", [P, 512])

        s_w = sem("weights_landed")
        s_item = sem("item_landed")
        s_const = sem("constants_set")
        s_id = sem("identity_ready")
        s_wT = sem("weights_transposed")
        s_wTc = sem("weightsT_copied")
        s_it = sem("item_transposed")
        s_itc = sem("itemT_copied")
        s_h = sem("h_computed")
        s_hc = sem("h_copied")
        s_y2 = sem("y_feat_landed")
        s_ones = sem("ones_set")
        s_yst = [sem(f"y_stored{b}") for b in range(2)]
        s_x1st = [sem(f"x1_stored{b}") for b in range(2)]
        L = [dict(
            adj=[sem(f"adj_landed{l}{b}") for b in range(2)],
            xin=[sem(f"xin_landed{l}{b}") for b in range(2)],
            tr=[sem(f"transposed{l}{b}") for b in range(2)],
            cp=[sem(f"copied{l}{b}") for b in range(2)],
            mm=[sem(f"multiplied{l}{b}") for b in range(2)],
            xt=sem(f"x_transposed{l}"),
            xtc=sem(f"xT_copied{l}"),
            acc=sem(f"sum_ready{l}"),
            read=sem(f"sum_read{l}"),
            zm=sem(f"z_multiplied{l}"),
            steps=sem(f"vector_steps{l}"),
            var=sem(f"variance_ready{l}"),
            std=sem(f"std_ready{l}"),
            tile=[sem(f"tile_done{l}{b}") for b in range(2)],
        ) for l in range(2)]
        s_ost = [sem(f"out_stored{b}") for b in range(2)]

        def tiles(eng, body):
            for b in range(2):
                body(b, 0, b, b * P)
            with eng.Fori(1, PAIRS) as k:
                for b in range(2):
                    body(2 * k + b, k, b, k * (2 * P) + b * P)
            body(NT - 1, PAIRS, 0, TAIL0)

        block = ctx.enter_context(nc.Block())

        @block.sync
        def _(sp):
            sp.dma_start(w_raw[:, 0, :], W_item).then_inc(s_w, 16)
            sp.dma_start(w_raw[:, 1, :], W_user).then_inc(s_w, 16)
            sp.dma_start(W1sb[:, :], W1).then_inc(s_w, 16)
            sp.dma_start(b_rows[:, 0, :], b_item.rearrange("(a n) -> a n", a=1)).then_inc(s_w, 16)
            sp.dma_start(b_rows[:, 1, :], b_user.rearrange("(a n) -> a n", a=1)).then_inc(s_w, 16)
            iv = adj_rows[1][:, 0:NFULL * D].rearrange("p (b d) -> p b d", d=D)
            sp.dma_start(iv, item[0:NFULL * P, :].rearrange("(b p) d -> p b d", p=P)).then_inc(s_item, 16)
            sp.dma_start(adj_rows[0][0:REST, 0:D], item[NFULL * P:N, :]).then_inc(s_item, 16)

            for l in range(2):
                S = L[l]
                if l == 0:
                    sp.wait_ge(s_it, NT)
                else:
                    for b, n in ((0, PAIRS + 1), (1, PAIRS)):
                        sp.wait_ge(s_yst[b], 16 * n)
                        sp.wait_ge(s_x1st[b], 16 * n)
                    sp.dma_start(feat[:, 0:NFULL, 0:D],
                                 y_dram[0:NFULL * P, :].rearrange("(b p) d -> p b d", p=P)).then_inc(s_y2, 16)
                    sp.dma_start(feat[0:REST, NFULL, 0:D], y_dram[NFULL * P:N, :]).then_inc(s_y2, 16)

                def tile(t, k, b, r0):
                    sp.wait_ge(S["tile"][b], k)
                    sp.dma_start(adj_rows[b][:, :], adj[bass.ds(r0, P), :]).then_inc(S["adj"][b], 16)
                    src = x if l == 0 else x1_dram
                    sp.dma_start(xin[b][:, :], src[bass.ds(r0, P), :]).then_inc(S["xin"][b], 16)

                tiles(sp, tile)

        @block.gpsimd
        def _(pool):
            pool.memset(ident[:, :], 0.0).then_inc(s_const, 1)
            pool.memset(feat[:, :, D:C], 1.0).then_inc(s_ones, 1)
            pool.memset(ones[:, :], 1.0).then_inc(s_ones, 1)
            pool.wait_ge(s_const, 1)
            pool.affine_select(out=ident[:, :], in_=ident[:, :], compare_op=ALU.not_equal, fill=1.0,
                               base=0, pattern=[[-1, P]], channel_multiplier=1).then_inc(s_id, 1)

            def store1(t, k, b, r0):
                pool.wait_ge(L[0]["tile"][b], k + 1)
                if r0 is TAIL0:
                    pool.wait_ge(s_x1st[1], 16 * PAIRS)
                    pool.wait_ge(s_yst[1], 16 * PAIRS)
                pool.dma_start(x1_dram[bass.ds(r0, P), :], x1[b][:, :]).then_inc(s_x1st[b], 16)
                pool.dma_start(y_dram[bass.ds(r0, P), :], y[b][:, :]).then_inc(s_yst[b], 16)

            tiles(pool, store1)

            def store2(t, k, b, r0):
                pool.wait_ge(L[1]["tile"][b], k + 1)
                if r0 is TAIL0:
                    pool.wait_ge(s_ost[1], 16 * PAIRS)
                pool.dma_start(out[bass.ds(r0, P), :], x1[b][:, :]).then_inc(s_ost[b], 16)

            tiles(pool, store2)
            pool.wait_ge(s_ost[0], 16 * (PAIRS + 1))
            pool.wait_ge(s_ost[1], 16 * PAIRS)

        @block.tensor
        def _(pe):
            pe.wait_ge(s_w, 80)
            pe.wait_ge(s_id, 1)
            pe.wait_ge(s_ones, 2)
            for i in range(2):
                nc.tensor.transpose((psX, psZ)[i][:, 0:P], w_raw[:, i, :], ident[:, :]).then_inc(s_wT, 1)
            pe.wait_ge(s_wTc, 2)
            pe.wait_ge(s_item, 32)

            def h_block(b, src, w):
                pe.wait_ge(s_itc, b)
                nc.tensor.transpose(psT[0][:, 0:w], src, ident[0:w, 0:w]).then_inc(s_it, 1)
                pe.wait_ge(s_itc, b + 1)
                pe.wait_ge(s_hc, b)
                nc.tensor.matmul(psO[0:w, 0:D], xT[:, 0:w], WiT[:, :], start=True, stop=False)
                nc.tensor.matmul(psO[0:w, 0:D], ones[0:1, 0:w], b_rows[0:1, 0, :], start=False, stop=True).then_inc(s_h, 1)

            for b in range(NFULL):
                h_block(b, adj_rows[1][:, b * D:(b + 1) * D], P)
            h_block(NFULL, adj_rows[0][0:REST, 0:D], REST)
            pe.wait_ge(s_hc, NT)

            for l in range(2):
                S = L[l]
                if l == 1:
                    pe.wait_ge(s_y2, 32)

                def tile(t, k, b, r0):
                    pe.wait_ge(S["adj"][b], 16 * (k + 1))
                    if l == 0:
                        pe.wait_ge(S["xin"][b], 16 * (k + 1))
                        nc.tensor.transpose(psX[:, 0:P], xin[b][:, :], ident[:, :]).then_inc(S["xt"], 1)

                    def transposes(g):
                        e = g % 2
                        pe.wait_ge(S["cp"][e], t * HG + g // 2)
                        for i, c in enumerate(groups[g]):
                            w = widths[c]
                            last = nc.tensor.transpose(psT[e][0:w, i * P:(i + 1) * P],
                                                       adj_rows[b][:, c * P:c * P + w], ident[:, :])
                        last.then_inc(S["tr"][e], 1)

                    def products(g):
                        e = g % 2
                        pe.wait_ge(S["cp"][e], t * HG + g // 2 + 1)
                        if g == 0 and l == 0:
                            pe.wait_ge(S["read"], t)
                        for i, c in enumerate(groups[g]):
                            w = widths[c]
                            last = nc.tensor.matmul(psO[:, 0:C], adjT[e][0:w, i * P:(i + 1) * P], feat[0:w, c, :],
                                                    start=(c == 0), stop=(l == 1 and c == NT - 1))
                        last.then_inc(S["mm"][e], 1)

                    transposes(0)
                    for g in range(NG):
                        if g + 1 < NG:
                            transposes(g + 1)
                        products(g)
                    if l == 0:
                        pe.wait_ge(S["xtc"], t + 1)
                        nc.tensor.matmul(psO[:, 0:D], xT[:, :], WuT[:, :], start=False, stop=False)
                        nc.tensor.matmul(psO[:, 0:D], ones[0:1, :], b_rows[0:1, 1, :], start=False, stop=True).then_inc(S["acc"], 1)
                    else:
                        pe.wait_ge(S["steps"], t * 5 + 1)
                        nc.tensor.transpose(psX[:, 0:P], zs[:, :], ident[:, :]).then_inc(S["xt"], 1)
                        pe.wait_ge(S["xtc"], t + 1)
                        nc.tensor.matmul(psZ[:, 0:D], xT[:, :], W1sb[:, :], start=True, stop=True).then_inc(S["zm"], 1)

                tiles(pe, tile)

        @block.scalar
        def _(act):
            for i, dst in enumerate((WiT, WuT)):
                act.wait_ge(s_wT, i + 1)
                nc.scalar.copy(dst[:, :], (psX, psZ)[i][:, 0:P]).then_inc(s_wTc, 1)
            for b in range(NT):
                w = widths[b]
                act.wait_ge(s_it, b + 1)
                act.wait_ge(s_h, b)
                nc.scalar.copy(xT[:, 0:w], psT[0][:, 0:w]).then_inc(s_itc, 1)

            for l in range(2):
                S = L[l]

                def tile(t, k, b, r0):
                    def copy_xT():
                        act.wait_ge(S["xt"], t + 1)
                        act.wait_ge(S["acc"] if l == 0 else S["zm"], t)
                        nc.scalar.copy(xT[:, :], psX[:, 0:P]).then_inc(S["xtc"], 1)

                    if l == 0:
                        copy_xT()
                    for g in range(0, NG, 2):
                        act.wait_ge(S["tr"][0], t * HG + g // 2 + 1)
                        act.wait_ge(S["mm"][0], t * HG + g // 2)
                        nc.scalar.copy(adjT[0][:, :], psT[0][:, :]).then_inc(S["cp"][0], 1)
                    if l == 1:
                        copy_xT()
                    act.wait_ge(S["var"], t + 1)
                    n = 2 if l == 0 else 1
                    nc.scalar.activation(sq[:, 0:n], mv[:, 1:1 + n], ACT.Sqrt).then_inc(S["std"], 1)

                tiles(act, tile)

        @block.vector
        def _(dve):
            for b in range(NT):
                w = widths[b]
                dve.wait_ge(s_h, b + 1)
                nc.vector.tensor_copy(feat[0:w, b, 0:D], psO[0:w, 0:D]).then_inc(s_hc, 1)

            for l in range(2):
                S = L[l]
                if l == 1:
                    dve.wait_ge(s_x1st[0], 16 * (PAIRS + 1))
                    dve.wait_ge(s_x1st[1], 16 * PAIRS)

                def tile(t, k, b, r0):
                    for g in range(1, NG, 2):
                        dve.wait_ge(S["tr"][1], t * HG + g // 2 + 1)
                        dve.wait_ge(S["mm"][1], t * HG + g // 2)
                        nc.vector.tensor_copy(adjT[1][:, :], psT[1][:, :]).then_inc(S["cp"][1], 1)
                    step = [t * 5]

                    def chain(ins):
                        ins.then_inc(S["steps"], 1)
                        step[0] = step[0] + 1
                        dve.wait_ge(S["steps"], step[0])

                    if l == 0:
                        dve.wait_ge(S["acc"], t + 1)
                        chain(nc.vector.scalar_tensor_tensor(out=res[:, :], in0=psO[:, 0:D], scalar=0.0,
                                                             in1=xin[b][:, :], op0=ALU.max, op1=ALU.add))
                    else:
                        dve.wait_ge(S["mm"][1], (t + 1) * HG)
                        chain(nc.vector.tensor_scalar(zs[:, :], psO[:, 0:D], dinv[:, bass.ds(t, 1)], None, ALU.mult))
                        dve.wait_ge(S["zm"], t + 1)
                        dve.wait_ge(S["xin"][b], 16 * (k + 1))
                        chain(nc.vector.scalar_tensor_tensor(out=res[:, :], in0=psZ[:, 0:D], scalar=0.0,
                                                             in1=xin[b][:, :], op0=ALU.max, op1=ALU.add))
                    chain(nc.vector.bn_stats(stats[:, :], res[:, :]))
                    if l == 0:
                        nc.vector.tensor_copy(mv[:, 2:3], psO[:, D:C]).then_inc(S["read"], 1)
                    else:
                        nc.vector.tensor_copy(mv[:, 2:3], stats[:, 0:1])
                    chain(nc.vector.bn_aggr(mv[:, 0:2], stats[:, :]))
                    nc.vector.tensor_scalar_add(mv[:, 1:2], mv[:, 1:2], EPS).then_inc(S["var"], 1)
                    dve.wait_ge(S["std"], t + 1)
                    chain(nc.vector.reciprocal(rs[:, :], sq[:, :]))
                    if l == 0:
                        dve.wait_ge(s_x1st[b], 16 * k)
                        dve.wait_ge(s_yst[b], 16 * k)
                        nc.vector.tensor_copy(dinv[:, bass.ds(t, 1)], rs[:, 1:2])
                        chain(nc.vector.tensor_scalar(x1[b][:, :], res[:, :], mv[:, 0:1], rs[:, 0:1],
                                                      ALU.subtract, ALU.mult))
                        nc.vector.tensor_scalar(y[b][:, :], x1[b][:, :], rs[:, 1:2], None, ALU.mult
                                                ).then_inc(S["tile"][b], 1)
                    else:
                        dve.wait_ge(s_ost[b], 16 * k)
                        nc.vector.tensor_scalar(x1[b][:, :], res[:, :], mv[:, 0:1], rs[:, 0:1],
                                                ALU.subtract, ALU.mult).then_inc(S["tile"][b], 1)

                tiles(dve, tile)


_INS = ['x', 'adj', 'L0_gnn_item_feat', 'L0_gnn_W_item', 'L0_gnn_b_item', 'L0_gnn_W_user', 'L0_gnn_b_user', 'L1_gnn_W']
_OUTS = [((10000, 128), 'float32')]


def kernel(**inputs):
    import numpy as _np
    import concourse.bacc as _bacc
    from concourse import mybir as _mybir
    from concourse.bass_utils import run_bass_kernel_spmd as _run

    nc = _bacc.Bacc("TRN2", target_bir_lowering=False, num_devices=1)
    arrays, args = {}, []
    for name in _INS:
        a = _np.ascontiguousarray(inputs[name])
        arrays[f"in_{name}_dram"] = a
        args.append(nc.dram_tensor(f"in_{name}_dram", a.shape, _mybir.dt.from_np(a.dtype), kind="ExternalInput").ap())
    for i, (shape, dtype) in enumerate(_OUTS):
        dt = _mybir.dt.from_np(_np.dtype(dtype))
        args.append(nc.dram_tensor(f"out_{i}_dram", shape, dt, kind="ExternalOutput").ap())
    gnn_kernel(nc, *args)
    r = _run(nc, [arrays], core_ids=[0])
    return r.results[0]["out_0_dram"]
```

```python
from contextlib import ExitStack

import concourse.bass as bass
from concourse import mybir

P = 128
F32 = mybir.dt.float32
BF16 = mybir.dt.bfloat16
U32 = mybir.dt.uint32
I32 = mybir.dt.int32
ALU = mybir.AluOpType
ACT = mybir.ActivationFunctionType
AX_X = mybir.AxisListType.X
EPS = 1e-5

NB = 20
PIECES = 4
SLOTS = 16
CH = 4
LAG = 5
EXP_MASK = 0x7F800000
LOW = -1.0e9


def gnn_kernel(nc, x, adj, item, W_item, b_item, W_user, b_user, W1, out):
    N, D = x.shape
    assert D == P
    NT = -(-N // P)
    TAIL0 = N - P
    NFULL = N // P
    REST = N - NFULL * P
    PAIRS = (NT - 1) // 2
    assert NT == 2 * PAIRS + 1 and 0 < REST
    C = D + 1
    CW = N // NB
    HALF = CW // 2
    BPP = NB // PIECES
    PW = N // PIECES
    NE = CH * P
    NF = 2 + SLOTS
    assert CW * NB == N and NB % PIECES == 0 and NB <= 24 and CW <= 512

    x1_dram = nc.dram_tensor("x1_scratch", (N, D), F32, kind="Internal").ap()
    y_dram = nc.dram_tensor("y_scratch", (N, D), F32, kind="Internal").ap()
    adj_flat = adj.rearrange("a (b o) -> (a b) o", o=1)

    with ExitStack() as ctx:
        def sb(name, shape, dt=F32):
            return ctx.enter_context(nc.sbuf_tensor(name, shape, dt))

        def ps(name, shape, dt=F32):
            return ctx.enter_context(nc.psum_tensor(name, shape, dt))

        def sem(name):
            return ctx.enter_context(nc.semaphore(name))

        adj_rows = [sb(f"adj_rows{b}", [P, N]) for b in range(2)]
        feat = sb("feat", [P, NT, C])
        xall = feat[:, :, 0:D]
        signs = [sb(f"signs{p}", [P, PW], BF16) for p in range(PIECES)]
        sgn = [sb(f"sgn{b}", [P, PIECES]) for b in range(2)]
        pow2 = sb("pow2", [P, NB, P], BF16)
        ident = sb("ident", [P, P])
        before = sb("before", [P, P])
        shift = sb("shift", [P, P])
        delta = sb("delta", [P, P])
        iota_i = sb("iota_i", [P, NE], I32)
        iota_e = sb("iota_e", [P, NE])
        entry_no = sb("entry_no", [P, CH])
        halves = sb("halves", [P, SLOTS])
        top = [sb(f"top{b}", [P, SLOTS]) for b in range(2)]
        cidx = sb("cidx", [P, SLOTS], U32)
        cbase = sb("cbase", [P, SLOTS])
        masks3 = sb("masks3", [P, 3, SLOTS])
        high = sb("high", [P, SLOTS])
        expo = sb("expo", [P, 3, SLOTS], I32)
        keys = sb("keys", [P, 3, SLOTS])
        keys2 = sb("keys2", [P, 3, SLOTS])
        picked = sb("picked", [P, SLOTS])
        junk16 = sb("junk16", [P, SLOTS])
        rowcodes = [sb(f"rowcodes{b}", [P, 1 + SLOTS]) for b in range(2)]
        lowest = sb("lowest", [P, 1])
        sgnsum = sb("sgnsum", [P, 1])
        bad = sb("bad", [P, 1])
        most = sb("most", [P, 1])
        steps_m = sb("steps_m", [P, NE])
        fields = [sb(f"fields{b}", [P, NF]) for b in range(2)]
        slot = sb("slot", [P, CH])
        hit = sb("hit", [P, CH, SLOTS])
        code = sb("code", [P, CH])
        col = sb("col", [P, CH])
        jix = [sb(f"jix{b}", [P, CH], U32) for b in range(4)]
        rel = [sb(f"rel{b}", [P, CH], U32) for b in range(2)]
        vix = [sb(f"vix{b}", [P, CH], U32) for b in range(2)]
        tile_base = [sb(f"tile_base{b}", [P, CH], U32) for b in range(2)]
        pair_step = sb("pair_step", [P, CH], U32)
        jall = sb("jall", [P, NT * CH], U32)
        rall = sb("rall", [P, NT * CH])
        vall = sb("vall", [P, NT * CH])
        valid = sb("valid", [P, NT * CH])
        vraw = [sb(f"vraw{b}", [P, CH]) for b in range(2)]
        G = [sb(f"G{b}", [P, CH, P]) for b in range(4)]
        M = [sb(f"M{b}", [P, CH, P]) for b in range(2)]
        xs = sb("xs", [P, D])
        xT = sb("xT", [P, P])
        aggT = sb("aggT", [P, P])
        rs2 = sb("rs2", [2, P])
        bias2 = sb("bias2", [2, C])
        ones_col = sb("ones_col", [P, 1])
        w_raw = sb("w_raw", [P, 2, D])
        WiT = sb("WiT", [P, D])
        WuT = sb("WuT", [P, D])
        W1sb = sb("W1sb", [P, D])
        dinv = sb("dinv", [P, NT])
        stats = sb("stats", [P, 6])
        mv = [sb(f"mv{b}", [P, 3]) for b in range(2)]
        sq = [sb(f"sq{b}", [P, 2]) for b in range(2)]
        rs = [sb(f"rs{b}", [P, 2]) for b in range(2)]
        y = [sb(f"y{b}", [P, D]) for b in range(2)]
        zs = sb("zs", [P, D])
        res = [sb(f"res{b}", [P, D]) for b in range(2)]
        flag = sb("flag", [1, 1], I32)

        bank = [ps(f"bank{n}", [P, 512]) for n in range(8)]
        psM = bank[0:2]
        psS, psF, psA, psX, psZ, psW = bank[2:8]
        psF4 = psF[:, 0:CH * NF].rearrange("p (q f) -> p q f", f=NF)

        s_zero = sem("zeros_set")
        s_const = sem("constants_made")
        s_cst2 = sem("derived_constants_made")
        s_w = sem("weights_landed")
        s_x = sem("x_landed")
        s_wT = sem("weights_transposed")
        s_wTc = sem("weightsT_copied")
        s_adj = [[sem(f"adj_landed{b}{p}") for p in range(PIECES)] for b in range(2)]
        s_sign = [sem(f"signs_written{p}") for p in range(PIECES)]
        s_fold = [sem(f"signs_folded{p}") for p in range(PIECES)]
        s_mread = [sem(f"masks_read{b}") for b in range(2)]
        s_find = sem("find_steps")
        s_codes = sem("row_codes_ready")
        s_small = sem("offsets_ready")
        s_ent = sem("entry_steps")
        s_steps = sem("row_steps_ready")
        s_fld = sem("entry_fields_ready")
        s_idx = sem("indices_ready")
        s_vix = sem("value_indices_ready")
        s_vg = [sem(f"values_gathered{b}") for b in range(2)]
        s_G = [sem(f"rows_gathered{b}") for b in range(2)]
        s_val = sem("values_masked")
        s_M = sem("scatter_ready")
        s_xs = sem("x_tile_copied")
        s_xt = sem("x_transposed")
        s_xTc = sem("xT_copied")
        s_agg = sem("aggregate_ready")
        s_aggc = sem("aggregate_copied")
        s_z = sem("z_ready")
        s_ep1 = sem("residual_steps")
        s_var = sem("variance_ready")
        s_std = sem("std_ready")
        s_ep2 = sem("norm_steps")
        s_y = [sem(f"y_ready{b}") for b in range(2)]
        s_yst = [sem(f"y_stored{b}") for b in range(2)]
        s_fin2 = sem("norm_chain")
        s_fin = sem("flag_steps")
        s_flagp = sem("flag_summed")
        s_flag = sem("flag_ready")

        s2_turn = sem("gather2_turns")
        s2_jix = sem("list_indices_copied")
        s2_G = [sem(f"y_rows_gathered{b}") for b in range(2)]
        s2_M = sem("scatter2_ready")
        s2_agg = sem("aggregate2_ready")
        s2_aggc = sem("aggregate2_copied")
        s2_z = sem("z2_ready")
        s2_ep1 = sem("residual2_steps")
        s2_var = sem("variance2_ready")
        s2_std = sem("std2_ready")
        s2_n = sem("norm2_steps")
        s2_o = [sem(f"out_ready{b}") for b in range(2)]
        s2_ost = [sem(f"out_stored{b}") for b in range(2)]

        GB = 4
        widths = [P] * NFULL + [REST]
        groups = [list(range(g, min(g + GB, NT))) for g in range(0, NT, GB)]
        NG = len(groups)
        assert NG % 2 == 0
        HG = NG // 2
        blkT = [G[b][:, :, :].rearrange("p a b -> p (a b)") for b in range(2)]
        xin = [M[b][:, 0, :] for b in range(2)]
        resd = M[0][:, 1, :]
        x1d = [M[b][:, 2, :] for b in range(2)]
        pick = sb("pick", [2, 2, P])
        d_sel = sem("d_pick_made")
        d_ones = sem("d_ones_set")
        d_item = sem("d_item_landed")
        d_it = sem("d_item_transposed")
        d_itc = sem("d_itemT_copied")
        d_h = sem("d_h_computed")
        d_hc = sem("d_h_copied")
        d_y2 = sem("d_y_landed")
        d_yst = [sem(f"d_y_stored{b}") for b in range(2)]
        d_x1st = [sem(f"d_x1_stored{b}") for b in range(2)]
        d_ost = [sem(f"d_out_stored{b}") for b in range(2)]
        L = [dict(
            adj=[sem(f"d_adj_landed{l}{b}") for b in range(2)],
            xin=[sem(f"d_x_landed{l}{b}") for b in range(2)],
            tr=[sem(f"d_transposed{l}{b}") for b in range(2)],
            cp=[sem(f"d_copied{l}{b}") for b in range(2)],
            mm=[sem(f"d_multiplied{l}{b}") for b in range(2)],
            xt=sem(f"d_x_transposed{l}"),
            xtc=sem(f"d_xT_copied{l}"),
            acc=sem(f"d_sum_ready{l}"),
            read=sem(f"d_sum_read{l}"),
            zm=sem(f"d_z_multiplied{l}"),
            steps=sem(f"d_vector_steps{l}"),
            var=sem(f"d_variance_ready{l}"),
            std=sem(f"d_std_ready{l}"),
            tile=[sem(f"d_tile_done{l}{b}") for b in range(2)],
        ) for l in range(2)]

        def tiles(eng, body):
            for b in range(2):
                body(b, 0, b, b * P)
            with eng.Fori(1, PAIRS) as k:
                for b in range(2):
                    body(2 * k + b, k, b, k * (2 * P) + b * P)
            body(NT - 1, PAIRS, 0, TAIL0)

        def stage(k, b, lag):
            kk = k + (b - lag) // 2
            pp = (b - lag) % 2
            return 2 * kk + pp, kk, pp

        def row0(t):
            return min(t * P, TAIL0) if isinstance(t, int) else t * P

        def live(t):
            return not isinstance(t, int) or 0 <= t < NT

        def iterations(eng, body, lag):
            head = -(-lag // 2) * 2
            for i in range(head):
                body(i // 2, i % 2)
            with eng.Fori(head // 2, PAIRS) as k:
                for b in range(2):
                    body(k, b)
            for i in range(2 * PAIRS, NT + lag):
                body(i // 2, i % 2)

        NCONST = 5
        NCST2 = 4

        block = ctx.enter_context(nc.Block())

        @block.sync
        def _(sp):
            def load(k, b, r0):
                for p in range(PIECES):
                    sp.wait_ge(s_sign[p], 2 * k + b - 1 if not isinstance(k, int) or k else 0)
                    sp.dma_start(adj_rows[b][:, p * PW:(p + 1) * PW],
                                 adj[bass.ds(r0, P), p * PW:(p + 1) * PW]).then_inc(s_adj[b][p], 16)

            load(0, 0, 0)
            sp.dma_start(w_raw[:, 0, :], W_item).then_inc(s_w, 16)
            sp.dma_start(w_raw[:, 1, :], W_user).then_inc(s_w, 16)
            sp.dma_start(W1sb[:, :], W1).then_inc(s_w, 16)
            sp.wait_ge(s_const, NCONST)
            sp.dma_start(bias2[0:1, 0:D], b_item.rearrange("(a n) -> a n", a=1)).then_inc(s_w, 16)
            sp.dma_start(bias2[1:2, 0:D], b_user.rearrange("(a n) -> a n", a=1)).then_inc(s_w, 16)
            load(0, 1, P)
            sp.dma_start(xall[:, 0:NFULL, :],
                         x[0:NFULL * P, :].rearrange("(b p) d -> p b d", p=P)).then_inc(s_x, 16)
            sp.dma_start(xall[:, NFULL, :], x[TAIL0:N, :]).then_inc(s_x, 16)
            with sp.Fori(1, PAIRS) as k:
                for b in range(2):
                    load(k, b, k * (2 * P) + b * P)
            load(PAIRS, 0, TAIL0)

            sp.wait_ge(s_flag, 1)
            faults = sp.value_load(flag[0:1, 0:1], min_val=0, max_val=1 << 20)
            with sp.If(faults != 0):
                iv = adj_rows[1][:, 0:NFULL * D].rearrange("p (b d) -> p b d", d=D)
                sp.dma_start(iv, item[0:NFULL * P, :].rearrange("(b p) d -> p b d", p=P)).then_inc(d_item, 16)
                sp.dma_start(adj_rows[0][0:REST, 0:D], item[NFULL * P:N, :]).then_inc(d_item, 16)

                for l in range(2):
                    S = L[l]
                    if l == 0:
                        sp.wait_ge(d_it, NT)
                    else:
                        for b, n in ((0, PAIRS + 1), (1, PAIRS)):
                            sp.wait_ge(d_yst[b], 16 * n)
                            sp.wait_ge(d_x1st[b], 16 * n)
                        sp.dma_start(feat[:, 0:NFULL, 0:D],
                                     y_dram[0:NFULL * P, :].rearrange("(b p) d -> p b d", p=P)).then_inc(d_y2, 16)
                        sp.dma_start(feat[0:REST, NFULL, 0:D], y_dram[NFULL * P:N, :]).then_inc(d_y2, 16)

                    def tile(t, k, b, r0):
                        sp.wait_ge(S["tile"][b], k)
                        sp.dma_start(adj_rows[b][:, :], adj[bass.ds(r0, P), :]).then_inc(S["adj"][b], 16)
                        src = x if l == 0 else x1_dram
                        sp.dma_start(xin[b], src[bass.ds(r0, P), :]).then_inc(S["xin"][b], 16)

                    tiles(sp, tile)


        @block.gpsimd
        def _(pool):
            pool.memset(ident[:, :], 0.0).then_inc(s_zero, 1)
            pool.memset(shift[:, :], 0.0).then_inc(s_zero, 1)
            pool.memset(before[:, :], 1.0).then_inc(s_zero, 1)
            pool.memset(ones_col[:, :], 1.0).then_inc(s_zero, 1)
            pool.memset(rs2[:, :], 1.0).then_inc(s_zero, 1)
            pool.memset(bias2[:, :], 0.0).then_inc(s_zero, 1)
            pool.memset(pair_step[:, :], 2 * P * N).then_inc(s_zero, 1)
            pool.memset(tile_base[0][:, :], 0).then_inc(s_zero, 1)
            pool.memset(tile_base[1][:, :], P * N).then_inc(s_zero, 1)
            pool.iota(iota_i[:, :], [[1, NE]], base=0, channel_multiplier=0).then_inc(s_zero, 1)
            pool.wait_ge(s_zero, 10)
            pool.affine_select(out=ident[:, :], in_=ident[:, :], compare_op=ALU.not_equal, fill=1.0,
                               base=0, pattern=[[-1, P]], channel_multiplier=1).then_inc(s_const, 1)
            pool.affine_select(out=shift[:, :], in_=shift[:, :], compare_op=ALU.not_equal, fill=1.0,
                               base=1, pattern=[[-1, P]], channel_multiplier=1).then_inc(s_const, 1)
            pool.affine_select(out=before[:, :], in_=before[:, :], compare_op=ALU.is_gt, fill=0.0,
                               base=0, pattern=[[1, P]], channel_multiplier=-1).then_inc(s_const, 1)
            pool.memset(bias2[0:1, D:C], 1.0).then_inc(s_const, 1)
            pool.iota(entry_no[:, :], [[P, CH]], base=0, channel_multiplier=1,
                      allow_small_or_imprecise_dtypes=True).then_inc(s_const, 1)

            def gather(k, b):
                t, kk, pp = stage(k, b, 2)
                if live(t):
                    pool.wait_ge(s_val, t - 1 if not isinstance(t, int) else max(t - 1, 0))
                    pool.wait_ge(s_idx, t + 1)
                    if isinstance(t, int) and t == NT - 1:
                        pool.memset(tile_base[pp][:, :], TAIL0 * N).then_inc(s_vix, 1)
                        pool.wait_ge(s_vix, 2 * t + 1)
                    pool.tensor_tensor(vix[pp][:, :], rel[pp][:, :], tile_base[pp][:, :], ALU.add).then_inc(s_vix, 1)
                    pool.wait_ge(s_vix, 2 * t + (2 if isinstance(t, int) and t == NT - 1 else 1))
                    pool.wait_ge(s_agg, t - 1 if not isinstance(t, int) else max(t - 1, 0))
                    pool.tensor_tensor(tile_base[pp][:, :], tile_base[pp][:, :], pair_step[:, :],
                                       ALU.add).then_inc(s_vix, 1)
                    for q in range(CH):
                        pool.indirect_dma_start(vraw[pp][:, q:q + 1], None, adj_flat,
                                                bass.IndirectOffsetOnAxis(ap=vix[pp][:, q:q + 1], axis=0)
                                                ).then_inc(s_vg[pp], 16)
                    for q in range(CH):
                        pool.indirect_dma_start(G[pp][:, q, :], None, item,
                                                bass.IndirectOffsetOnAxis(ap=jix[pp][:, q:q + 1], axis=0)
                                                ).then_inc(s_G[pp], 16)

            iterations(pool, gather, LAG)

            pool.wait_ge(s_flag, 1)
            faults = pool.value_load(flag[0:1, 0:1], min_val=0, max_val=1 << 20)
            with pool.If(faults == 0):
                pool.wait_ge(s_yst[0], 16 * (PAIRS + 1))
                pool.wait_ge(s_yst[1], 16 * PAIRS)

                def gather_y(k, b):
                    t, kk, pp = stage(k, b, 0)
                    if live(t):
                        pool.wait_ge(s2_agg, t - 1 if not isinstance(t, int) else max(t - 1, 0))
                        pool.wait_ge(s2_jix, t + 1)
                        pool.wait_ge(s2_turn, t)
                        pool.tensor_tensor(vix[pp][:, :], pair_step[:, :], pair_step[:, :], ALU.add).then_inc(s2_turn, 1)
                        for q in range(CH):
                            pool.indirect_dma_start(G[pp][:, q, :], None, y_dram,
                                                    bass.IndirectOffsetOnAxis(ap=jix[pp][:, q:q + 1], axis=0)
                                                    ).then_inc(s2_G[pp], 16)

                iterations(pool, gather_y, 4)
            with pool.Else():
                pool.wait_ge(s_yst[0], 16 * (PAIRS + 1))
                pool.wait_ge(s_yst[1], 16 * PAIRS)
                pool.memset(feat[:, :, D:C], 1.0).then_inc(d_ones, 1)

                def store1(t, k, b, r0):
                    pool.wait_ge(L[0]["tile"][b], k + 1)
                    if r0 is TAIL0:
                        pool.wait_ge(d_x1st[1], 16 * PAIRS)
                        pool.wait_ge(d_yst[1], 16 * PAIRS)
                    pool.dma_start(x1_dram[bass.ds(r0, P), :], x1d[b]).then_inc(d_x1st[b], 16)
                    pool.dma_start(y_dram[bass.ds(r0, P), :], y[b][:, :]).then_inc(d_yst[b], 16)

                tiles(pool, store1)

                def store2(t, k, b, r0):
                    pool.wait_ge(L[1]["tile"][b], k + 1)
                    if r0 is TAIL0:
                        pool.wait_ge(d_ost[1], 16 * PAIRS)
                    pool.dma_start(out[bass.ds(r0, P), :], x1d[b]).then_inc(d_ost[b], 16)

                tiles(pool, store2)
                pool.wait_ge(d_ost[0], 16 * (PAIRS + 1))
                pool.wait_ge(d_ost[1], 16 * PAIRS)


        @block.tensor
        def _(pe):
            pe.wait_ge(s_w, 80)
            pe.wait_ge(s_const, NCONST)
            for i, ps_w in enumerate((psX, psZ)):
                nc.tensor.transpose(ps_w[:, 0:P], w_raw[:, i, :], ident[:, :]).then_inc(s_wT, 1)
            pe.wait_ge(s_wTc, 2)
            pe.wait_ge(s_cst2, NCST2)

            def fold(t, pp, pieces):
                for p in pieces:
                    pe.wait_ge(s_sign[p], t + 1)
                    for j in range(BPP):
                        blk = p * BPP + j
                        last = nc.tensor.matmul(psM[pp][:, 0:CW], pow2[:, blk, :], signs[p][:, j * CW:(j + 1) * CW],
                                                start=(blk == 0), stop=(blk == NB - 1))
                    last.then_inc(s_fold[p], 1)

            def body(k, b):
                t, kk, pp = stage(k, b, 1)
                if live(t):
                    pe.wait_ge(s_codes, t + 1)
                    nc.tensor.matmul(psS[:, 0:1], before[:, :], rowcodes[pp][:, 0:1], start=True, stop=True)
                    nc.tensor.matmul(psS[:, 1:2], shift[:, :], rowcodes[pp][:, 0:1], start=True, stop=True)
                    nc.tensor.matmul(psS[:, 2:NF], delta[:, :], rowcodes[pp][:, 1:1 + SLOTS],
                                     start=True, stop=True).then_inc(s_small, 1)
                t, kk, pp = stage(k, b, 3)
                if live(t):
                    pe.wait_ge(s_xs, t + 1)
                    nc.tensor.transpose(psX[:, 0:P], xs[:, :], ident[:, :]).then_inc(s_xt, 1)
                    pe.wait_ge(s_M, t + 1)
                    pe.wait_ge(s_G[pp], 16 * CH * (kk + 1))
                    for q in range(CH):
                        nc.tensor.matmul(psA[:, 0:P], G[pp][:, q, :], M[pp][:, q, :],
                                         start=(q == 0), stop=(q == CH - 1))
                    for q in range(CH):
                        last = nc.tensor.matmul(psA[0:1, P:2 * P], ones_col[:, :], M[pp][:, q, :],
                                                start=(q == 0), stop=(q == CH - 1))
                    last.then_inc(s_agg, 1)
                t0, k0, p0 = stage(k, b, 0)
                if live(t0):
                    pe.wait_ge(s_mread[p0], k0)
                    fold(t0, p0, range(0, PIECES // 2))
                if live(t):
                    pe.wait_ge(s_aggc, t + 1)
                    pe.wait_ge(s_var, t)
                    nc.tensor.matmul(psZ[:, 0:C], rs2[:, :], bias2[:, :], start=True, stop=False)
                    nc.tensor.matmul(psZ[:, 0:D], xT[:, :], WuT[:, :], start=False, stop=False)
                    nc.tensor.matmul(psZ[:, 0:D], aggT[:, :], WiT[:, :], start=False, stop=True).then_inc(s_z, 1)
                t, kk, pp = stage(k, b, 1)
                if live(t):
                    pe.wait_ge(s_steps, t + 1)
                    for q in range(CH):
                        last = nc.tensor.matmul(psF4[:, q, :], steps_m[:, q * P:(q + 1) * P], fields[pp][:, :],
                                                start=True, stop=True)
                    last.then_inc(s_fld, 1)
                if live(t0):
                    fold(t0, p0, range(PIECES // 2, PIECES))

            iterations(pe, body, LAG)
            pe.wait_ge(s_fin, 1)
            nc.tensor.matmul(psS[0:1, 0:1], bad[:, :], ones_col[:, :], start=True, stop=True).then_inc(s_flagp, 1)

            pe.wait_ge(s_flag, 1)
            faults = pe.value_load(flag[0:1, 0:1], min_val=0, max_val=1 << 20)
            with pe.If(faults == 0):
                def body2(k, b):
                    t, kk, pp = stage(k, b, 1)
                    if live(t):
                        pe.wait_ge(s2_M, t + 1)
                        pe.wait_ge(s2_G[pp], 16 * CH * (kk + 1))
                        for q in range(CH):
                            last = nc.tensor.matmul(psA[:, 0:P], G[pp][:, q, :], M[pp][:, q, :],
                                                    start=(q == 0), stop=(q == CH - 1))
                        last.then_inc(s2_agg, 1)
                        pe.wait_ge(s2_aggc, t + 1)
                        pe.wait_ge(s2_var, t)
                        nc.tensor.matmul(psW[:, 0:D], aggT[:, :], W1sb[:, :], start=True, stop=True).then_inc(s2_z, 1)

                iterations(pe, body2, 4)
            with pe.Else():
                pe.wait_ge(d_ones, 1)
                pe.wait_ge(d_sel, 1)
                pe.wait_ge(d_item, 32)

                def h_block(b, src, w):
                    pe.wait_ge(d_itc, b)
                    nc.tensor.transpose(psM[0][:, 0:w], src, ident[0:w, 0:w]).then_inc(d_it, 1)
                    pe.wait_ge(d_itc, b + 1)
                    pe.wait_ge(d_hc, b)
                    nc.tensor.matmul(psZ[0:w, 0:D], xT[:, 0:w], WiT[:, :], start=True, stop=False)
                    nc.tensor.matmul(psZ[0:w, 0:D], pick[:, 0, 0:w], bias2[:, 0:D], start=False, stop=True).then_inc(d_h, 1)

                for b in range(NFULL):
                    h_block(b, adj_rows[1][:, b * D:(b + 1) * D], P)
                h_block(NFULL, adj_rows[0][0:REST, 0:D], REST)
                pe.wait_ge(d_hc, NT)

                for l in range(2):
                    S = L[l]
                    if l == 1:
                        pe.wait_ge(d_y2, 32)

                    def tile(t, k, b, r0):
                        pe.wait_ge(S["adj"][b], 16 * (k + 1))
                        if l == 0:
                            pe.wait_ge(S["xin"][b], 16 * (k + 1))
                            nc.tensor.transpose(psX[:, 0:P], xin[b], ident[:, :]).then_inc(S["xt"], 1)

                        def transposes(g):
                            e = g % 2
                            pe.wait_ge(S["cp"][e], t * HG + g // 2)
                            for i, c in enumerate(groups[g]):
                                w = widths[c]
                                last = nc.tensor.transpose(psM[e][0:w, i * P:(i + 1) * P],
                                                           adj_rows[b][:, c * P:c * P + w], ident[:, :])
                            last.then_inc(S["tr"][e], 1)

                        def products(g):
                            e = g % 2
                            pe.wait_ge(S["cp"][e], t * HG + g // 2 + 1)
                            if g == 0 and l == 0:
                                pe.wait_ge(S["read"], t)
                            for i, c in enumerate(groups[g]):
                                w = widths[c]
                                last = nc.tensor.matmul(psZ[:, 0:C], blkT[e][0:w, i * P:(i + 1) * P], feat[0:w, c, :],
                                                        start=(c == 0), stop=(l == 1 and c == NT - 1))
                            last.then_inc(S["mm"][e], 1)

                        transposes(0)
                        for g in range(NG):
                            if g + 1 < NG:
                                transposes(g + 1)
                            products(g)
                        if l == 0:
                            pe.wait_ge(S["xtc"], t + 1)
                            nc.tensor.matmul(psZ[:, 0:D], xT[:, :], WuT[:, :], start=False, stop=False)
                            nc.tensor.matmul(psZ[:, 0:D], pick[:, 1, :], bias2[:, 0:D], start=False, stop=True).then_inc(S["acc"], 1)
                        else:
                            pe.wait_ge(S["steps"], t * 5 + 1)
                            nc.tensor.transpose(psX[:, 0:P], zs[:, :], ident[:, :]).then_inc(S["xt"], 1)
                            pe.wait_ge(S["xtc"], t + 1)
                            nc.tensor.matmul(psW[:, 0:D], xT[:, :], W1sb[:, :], start=True, stop=True).then_inc(S["zm"], 1)

                    tiles(pe, tile)


        @block.scalar
        def _(act):
            def sign(t, k, b, pieces):
                for p in pieces:
                    act.wait_ge(s_adj[b][p], 16 * (k + 1))
                    if p == 0:
                        act.wait_ge(s_codes, t - 1 if not isinstance(t, int) else max(t - 1, 0))
                    act.wait_ge(s_fold[p], t)
                    nc.scalar.activation(signs[p][:, :], adj_rows[b][:, p * PW:(p + 1) * PW], ACT.Sign,
                                         accum_out=sgn[b][:, p:p + 1]).then_inc(s_sign[p], 1)

            sign(0, 0, 0, range(PIECES))
            for i, (dst, ps_w) in enumerate(((WiT, psX), (WuT, psZ))):
                act.wait_ge(s_wT, i + 1)
                nc.scalar.copy(dst[:, :], ps_w[:, 0:P]).then_inc(s_wTc, 1)

            def body(k, b):
                t, kk, pp = stage(k, b, 5)
                if live(t):
                    act.wait_ge(s_y[pp], kk + 1)
                    if isinstance(t, int) and t == NT - 1:
                        act.wait_ge(s_yst[1], 16 * PAIRS)
                    act.dma_start(y_dram[bass.ds(row0(t), P), :], y[pp][:, :]).then_inc(s_yst[pp], 16)
                t, kk, pp = stage(k, b, 3)
                if live(t):
                    if isinstance(t, int) and t == 0:
                        act.wait_ge(s_x, 32)
                    act.wait_ge(s_wTc, 2)
                    act.wait_ge(s_xt, t)
                    nc.scalar.copy(xs[:, :], xall[:, t, :]).then_inc(s_xs, 1)
                t0, k0, p0 = stage(k, b, 0)
                first = isinstance(t0, int) and t0 == 0
                if live(t0) and not first:
                    sign(t0, k0, p0, range(0, PIECES // 2))
                if live(t):
                    act.wait_ge(s_xt, t + 1)
                    act.wait_ge(s_z, t)
                    nc.scalar.copy(xT[:, :], psX[:, 0:P]).then_inc(s_xTc, 1)
                    act.wait_ge(s_agg, t + 1)
                    nc.scalar.copy(aggT[:, :], psA[:, 0:P])
                    nc.scalar.copy(rs2[0:1, :], psA[0:1, P:2 * P]).then_inc(s_aggc, 1)
                if live(t0) and not first:
                    sign(t0, k0, p0, range(PIECES // 2, PIECES))
                t, kk, pp = stage(k, b, 4)
                if live(t):
                    act.wait_ge(s_ep2, t - 1 if not isinstance(t, int) else max(t - 1, 0))
                    act.wait_ge(s_var, t + 1)
                    nc.scalar.activation(sq[pp][:, :], mv[pp][:, 1:3], ACT.Sqrt).then_inc(s_std, 1)

            iterations(act, body, LAG)
            act.wait_ge(s_yst[0], 16 * (PAIRS + 1))
            act.wait_ge(s_yst[1], 16 * PAIRS)

            act.wait_ge(s_flag, 1)
            faults = act.value_load(flag[0:1, 0:1], min_val=0, max_val=1 << 20)
            with act.If(faults == 0):
                def body2(k, b):
                    t, kk, pp = stage(k, b, 1)
                    if live(t):
                        act.wait_ge(s2_agg, t + 1)
                        act.wait_ge(s2_z, t)
                        nc.scalar.copy(aggT[:, :], psA[:, 0:P]).then_inc(s2_aggc, 1)
                    t, kk, pp = stage(k, b, 2)
                    if live(t):
                        act.wait_ge(s2_n, t - 1 if not isinstance(t, int) else max(t - 1, 0))
                        act.wait_ge(s2_var, t + 1)
                        nc.scalar.activation(sq[pp][:, 0:1], mv[pp][:, 1:2], ACT.Sqrt).then_inc(s2_std, 1)
                    t, kk, pp = stage(k, b, 4)
                    if live(t):
                        act.wait_ge(s2_o[pp], kk + 1)
                        if isinstance(t, int) and t == NT - 1:
                            act.wait_ge(s2_ost[1], 16 * PAIRS)
                        act.dma_start(out[bass.ds(row0(t), P), :], y[pp][:, :]).then_inc(s2_ost[pp], 16)

                iterations(act, body2, 4)
                act.wait_ge(s2_ost[0], 16 * (PAIRS + 1))
                act.wait_ge(s2_ost[1], 16 * PAIRS)
            with act.Else():
                for b in range(NT):
                    w = widths[b]
                    act.wait_ge(d_it, b + 1)
                    act.wait_ge(d_h, b)
                    nc.scalar.copy(xT[:, 0:w], psM[0][:, 0:w]).then_inc(d_itc, 1)

                for l in range(2):
                    S = L[l]

                    def tile(t, k, b, r0):
                        def copy_xT():
                            act.wait_ge(S["xt"], t + 1)
                            act.wait_ge(S["acc"] if l == 0 else S["zm"], t)
                            nc.scalar.copy(xT[:, :], psX[:, 0:P]).then_inc(S["xtc"], 1)

                        if l == 0:
                            copy_xT()
                        for g in range(0, NG, 2):
                            act.wait_ge(S["tr"][0], t * HG + g // 2 + 1)
                            act.wait_ge(S["mm"][0], t * HG + g // 2)
                            nc.scalar.copy(blkT[0], psM[0][:, :]).then_inc(S["cp"][0], 1)
                        if l == 1:
                            copy_xT()
                        act.wait_ge(S["var"], t + 1)
                        n = 2 if l == 0 else 1
                        nc.scalar.activation(sq[0][:, 0:n], mv[0][:, 1:1 + n], ACT.Sqrt).then_inc(S["std"], 1)

                    tiles(act, tile)


        @block.vector
        def _(dve):
            def linker(semaphore, base):
                n = [base]

                def link(ins):
                    ins.then_inc(semaphore, 1)
                    n[0] = n[0] + 1
                    dve.wait_ge(semaphore, n[0])
                return link

            dve.wait_ge(s_zero, 10)
            dve.wait_ge(s_const, NCONST)
            nc.vector.memset(bad[:, :], 0.0)
            nc.vector.memset(most[:, :], 0.0)
            nc.vector.memset(halves[:, 0:8], -float(127 * CW - 1))
            nc.vector.memset(halves[:, 8:16], -float(127 * CW - 1 - HALF))
            nc.vector.tensor_copy(iota_e[:, :], iota_i[:, :]).then_inc(s_cst2, 1)
            nc.vector.tensor_tensor(delta[:, :], ident[:, :], shift[:, :], ALU.subtract).then_inc(s_cst2, 1)
            for blk in range(NB):
                last = nc.vector.tensor_scalar(pow2[:, blk, :], ident[:, :], float(2 ** blk), None, ALU.mult)
            last.then_inc(s_cst2, 1)
            for b in range(2):
                last = nc.vector.tensor_scalar(fields[b][:, 0:1], entry_no[:, 0:1], 1.0, None, ALU.min)
            last.then_inc(s_cst2, 1)
            dve.wait_ge(s_cst2, NCST2)

            def find(t, kk, pp):
                link = linker(s_find, t * 12)
                m = psM[pp][:, 0:CW]
                dve.wait_ge(s_fold[PIECES - 1], t + 1)
                nc.vector.tensor_reduce(lowest[:, :], m, AX_X, ALU.min)
                nc.vector.max(top[pp][:, 0:8], m[:, 0:HALF])
                link(nc.vector.max(top[pp][:, 8:16], m[:, HALF:CW]))
                nc.vector.tensor_scalar(masks3[:, 0, :], top[pp][:, :], 0.0, None, ALU.max)
                nc.vector.max_index(cidx[:, 0:8], top[pp][:, 0:8], m[:, 0:HALF])
                nc.vector.max_index(cidx[:, 8:16], top[pp][:, 8:16], m[:, HALF:CW]).then_inc(s_mread[pp], 1)
                dve.wait_ge(s_mread[pp], kk + 1)
                for lv in range(2):
                    link(nc.vector.tensor_scalar(high[:, :].bitcast(I32), masks3[:, lv, :].bitcast(I32), EXP_MASK,
                                                 None, ALU.bitwise_and))
                    link(nc.vector.tensor_tensor(masks3[:, lv + 1, :], masks3[:, lv, :], high[:, :], ALU.subtract))
                link(nc.vector.tensor_scalar(expo[:, :, :], masks3[:, :, :].bitcast(I32), 23, None,
                                             ALU.logical_shift_right))
                link(nc.vector.tensor_tensor(cbase[:, :], cidx[:, :], halves[:, :], ALU.add))
                link(nc.vector.scalar_tensor_tensor(out=keys[:, :, :], in0=expo[:, :, :], scalar=float(CW),
                                                    in1=cbase[:, :].unsqueeze(1).to_broadcast([P, 3, SLOTS]),
                                                    op0=ALU.mult, op1=ALU.add))
                nc.vector.tensor_reduce(sgnsum[:, :], sgn[pp][:, :], AX_X, ALU.add)
                link(nc.vector.max(picked[:, 0:8], keys[:, :, :]))
                nc.vector.tensor_scalar(rowcodes[pp][:, 1:9], picked[:, 0:8], 0.0, None, ALU.max)
                link(nc.vector.match_replace(keys2[:, :, :], picked[:, 0:8], keys[:, :, :], LOW))
                nc.vector.scalar_tensor_tensor(out=bad[:, :], in0=lowest[:, :], scalar=0.0, in1=bad[:, :],
                                               op0=ALU.is_lt, op1=ALU.add)
                link(nc.vector.max(picked[:, 8:16], keys2[:, :, :]))
                nc.vector.tensor_scalar(rowcodes[pp][:, 9:1 + SLOTS], picked[:, 8:16], 0.0, None, ALU.max)
                nc.vector.tensor_scalar(junk16[:, :], picked[:, :], 0.0, None, ALU.is_gt, ALU.add,
                                        accum_out=rowcodes[pp][:, 0:1]).then_inc(s_codes, 1)
                dve.wait_ge(s_codes, t + 1)
                link(nc.vector.scalar_tensor_tensor(out=bad[:, :], in0=sgnsum[:, :], scalar=rowcodes[pp][:, 0:1],
                                                    in1=bad[:, :], op0=ALU.not_equal, op1=ALU.add))

            def scatter(t, kk, pp):
                dve.wait_ge(s_vg[pp], 16 * CH * (kk + 1))
                dve.wait_ge(s_agg, t - 1 if not isinstance(t, int) else max(t - 1, 0))
                nc.vector.tensor_tensor(vall[:, bass.ds(t * CH, CH)], vraw[pp][:, :],
                                        valid[:, bass.ds(t * CH, CH)], ALU.mult).then_inc(s_val, 1)
                dve.wait_ge(s_val, t + 1)
                for q in range(CH):
                    last = nc.vector.tensor_scalar(M[pp][:, q, :], iota_e[:, 0:P], rall[:, bass.ds(t * CH + q, 1)],
                                                   vall[:, bass.ds(t * CH + q, 1)], ALU.is_equal, ALU.mult)
                last.then_inc(s_M, 1)

            def row_steps(t, kk, pp):
                link = linker(s_ent, t * 7)
                dve.wait_ge(s_small, t + 1)
                dve.wait_ge(s_fld, t)
                nc.vector.tensor_copy(fields[pp][:, 1:NF], psS[:, 1:NF])
                nc.vector.tensor_scalar(steps_m[:, :], iota_e[:, :], psS[:, 0:1], None, ALU.is_ge).then_inc(s_steps, 1)
                link(nc.vector.scalar_tensor_tensor(out=most[:, :], in0=psS[:, 0:1], scalar=rowcodes[pp][:, 0:1],
                                                    in1=most[:, :], op0=ALU.add, op1=ALU.max))

            def entries(t, kk, pp):
                link = linker(s_ent, t * 7 + 1)
                dve.wait_ge(s_fld, t + 1)
                link(nc.vector.tensor_tensor(slot[:, :], entry_no[:, :], psF4[:, :, 1], ALU.subtract))
                link(nc.vector.tensor_tensor(hit[:, :, :], slot[:, :].unsqueeze(2).to_broadcast([P, CH, SLOTS]),
                                             iota_e[:, 0:SLOTS].unsqueeze(1).to_broadcast([P, CH, SLOTS]),
                                             ALU.is_equal))
                link(nc.vector.tensor_tensor(hit[:, :, :], hit[:, :, :], psF4[:, :, 2:NF], ALU.mult))
                link(nc.vector.tensor_reduce(code[:, :], hit[:, :, :], AX_X, ALU.add))
                link(nc.vector.tensor_scalar(col[:, :], code[:, :], -1.0, 0.0, ALU.add, ALU.max))
                nc.vector.tensor_scalar(valid[:, bass.ds(t * CH, CH)], code[:, :], 1.0, None, ALU.min)
                nc.vector.tensor_copy(rall[:, bass.ds(t * CH, CH)], psF4[:, :, 0])
                nc.vector.tensor_copy(jall[:, bass.ds(t * CH, CH)], col[:, :])
                dve.wait_ge(s_G[pp], 16 * CH * kk)
                link(nc.vector.tensor_copy(jix[pp][:, :], col[:, :]))
                nc.vector.scalar_tensor_tensor(out=rel[pp][:, :], in0=psF4[:, :, 0], scalar=float(N),
                                               in1=col[:, :], op0=ALU.mult, op1=ALU.add).then_inc(s_idx, 1)
                dve.wait_ge(s_idx, t + 1)

            def residual(t, kk, pp):
                link = linker(s_ep1, t * 3)
                dve.wait_ge(s_z, t + 1)
                link(nc.vector.scalar_tensor_tensor(out=res[pp][:, :], in0=psZ[:, 0:D], scalar=0.0,
                                                    in1=xall[:, t, :], op0=ALU.max, op1=ALU.add))
                link(nc.vector.bn_stats(stats[:, :], res[pp][:, :]))
                nc.vector.tensor_copy(mv[pp][:, 2:3], psZ[:, D:C])
                link(nc.vector.bn_aggr(mv[pp][:, 0:2], stats[:, :]))
                nc.vector.tensor_scalar_add(mv[pp][:, 1:2], mv[pp][:, 1:2], EPS).then_inc(s_var, 1)

            def norm(t, kk, pp):
                link = linker(s_fin2, t * 2)
                dve.wait_ge(s_std, t + 1)
                link(nc.vector.reciprocal(rs[pp][:, :], sq[pp][:, :]))
                nc.vector.tensor_copy(dinv[:, bass.ds(t, 1)], rs[pp][:, 1:2]).then_inc(s_ep2, 1)
                link(nc.vector.tensor_scalar(xall[:, t, :], res[pp][:, :], mv[pp][:, 0:1], rs[pp][:, 0:1],
                                             ALU.subtract, ALU.mult))
                dve.wait_ge(s_yst[pp], 16 * kk)
                nc.vector.tensor_scalar(y[pp][:, :], xall[:, t, :], rs[pp][:, 1:2], None, ALU.mult).then_inc(s_y[pp], 1)

            def body(k, b):
                t1, k1, p1 = stage(k, b, 1)
                t3, k3, p3 = stage(k, b, 3)
                t4, k4, p4 = stage(k, b, 4)
                if live(t1):
                    find(t1, k1, p1)
                if live(t3):
                    scatter(t3, k3, p3)
                if live(t1):
                    row_steps(t1, k1, p1)
                if live(t3):
                    residual(t3, k3, p3)
                if live(t1):
                    entries(t1, k1, p1)
                if live(t4):
                    norm(t4, k4, p4)

            iterations(dve, body, LAG)
            nc.vector.scalar_tensor_tensor(out=bad[:, :], in0=most[:, :], scalar=float(NE), in1=bad[:, :],
                                           op0=ALU.is_gt, op1=ALU.add).then_inc(s_fin, 1)
            dve.wait_ge(s_flagp, 1)
            nc.vector.tensor_copy(flag[:, :], psS[0:1, 0:1]).then_inc(s_flag, 1)

            dve.wait_ge(s_flag, 1)
            faults = dve.value_load(flag[0:1, 0:1], min_val=0, max_val=1 << 20)
            with dve.If(faults == 0):
                dve.wait_ge(s_yst[0], 16 * (PAIRS + 1))
                dve.wait_ge(s_yst[1], 16 * PAIRS)

                def scatter2(t, kk, pp):
                    dve.wait_ge(s2_agg, t - 1 if not isinstance(t, int) else max(t - 1, 0))
                    for q in range(CH):
                        last = nc.vector.tensor_scalar(M[pp][:, q, :], iota_e[:, 0:P],
                                                       rall[:, bass.ds(t * CH + q, 1)],
                                                       vall[:, bass.ds(t * CH + q, 1)], ALU.is_equal, ALU.mult)
                    last.then_inc(s2_M, 1)

                def indices2(t, kk, pp):
                    dve.wait_ge(s2_G[pp], 16 * CH * kk)
                    nc.vector.tensor_copy(jix[pp][:, :], jall[:, bass.ds(t * CH, CH)]).then_inc(s2_jix, 1)

                def residual2(t, kk, pp):
                    link = linker(s2_ep1, t * 4)
                    dve.wait_ge(s2_z, t + 1)
                    link(nc.vector.tensor_scalar(zs[:, :], psW[:, 0:D], dinv[:, bass.ds(t, 1)], 0.0,
                                                 ALU.mult, ALU.max))
                    link(nc.vector.tensor_tensor(res[pp][:, :], xall[:, t, :], zs[:, :], ALU.add))
                    link(nc.vector.bn_stats(stats[:, :], res[pp][:, :]))
                    nc.vector.tensor_copy(mv[pp][:, 2:3], stats[:, 0:1])
                    link(nc.vector.bn_aggr(mv[pp][:, 0:2], stats[:, :]))
                    nc.vector.tensor_scalar_add(mv[pp][:, 1:2], mv[pp][:, 1:2], EPS).then_inc(s2_var, 1)

                def norm2(t, kk, pp):
                    dve.wait_ge(s2_std, t + 1)
                    nc.vector.reciprocal(rs[pp][:, 0:1], sq[pp][:, 0:1]).then_inc(s2_n, 1)
                    dve.wait_ge(s2_n, t + 1)
                    dve.wait_ge(s2_ost[pp], 16 * kk)
                    nc.vector.tensor_scalar(y[pp][:, :], res[pp][:, :], mv[pp][:, 0:1], rs[pp][:, 0:1],
                                            ALU.subtract, ALU.mult).then_inc(s2_o[pp], 1)

                def body2(k, b):
                    for lag, step in ((0, indices2), (1, scatter2), (2, residual2), (3, norm2)):
                        t, kk, pp = stage(k, b, lag)
                        if live(t):
                            step(t, kk, pp)

                iterations(dve, body2, 4)
            with dve.Else():
                dve.wait_ge(s_yst[0], 16 * (PAIRS + 1))
                dve.wait_ge(s_yst[1], 16 * PAIRS)
                for i in range(2):
                    last = nc.vector.tensor_copy(pick[:, i, :], ident[0:2, i:i + 1].to_broadcast([2, P]))
                last.then_inc(d_sel, 1)
                for b in range(NT):
                    w = widths[b]
                    dve.wait_ge(d_h, b + 1)
                    nc.vector.tensor_copy(feat[0:w, b, 0:D], psZ[0:w, 0:D]).then_inc(d_hc, 1)

                for l in range(2):
                    S = L[l]
                    if l == 1:
                        dve.wait_ge(d_x1st[0], 16 * (PAIRS + 1))
                        dve.wait_ge(d_x1st[1], 16 * PAIRS)

                    def tile(t, k, b, r0):
                        for g in range(1, NG, 2):
                            dve.wait_ge(S["tr"][1], t * HG + g // 2 + 1)
                            dve.wait_ge(S["mm"][1], t * HG + g // 2)
                            nc.vector.tensor_copy(blkT[1], psM[1][:, :]).then_inc(S["cp"][1], 1)
                        step = [t * 5]

                        def chain(ins):
                            ins.then_inc(S["steps"], 1)
                            step[0] = step[0] + 1
                            dve.wait_ge(S["steps"], step[0])

                        if l == 0:
                            dve.wait_ge(S["acc"], t + 1)
                            chain(nc.vector.scalar_tensor_tensor(out=resd, in0=psZ[:, 0:D], scalar=0.0,
                                                                 in1=xin[b], op0=ALU.max, op1=ALU.add))
                        else:
                            dve.wait_ge(S["mm"][1], (t + 1) * HG)
                            chain(nc.vector.tensor_scalar(zs[:, :], psZ[:, 0:D], dinv[:, bass.ds(t, 1)], None, ALU.mult))
                            dve.wait_ge(S["zm"], t + 1)
                            dve.wait_ge(S["xin"][b], 16 * (k + 1))
                            chain(nc.vector.scalar_tensor_tensor(out=resd, in0=psW[:, 0:D], scalar=0.0,
                                                                 in1=xin[b], op0=ALU.max, op1=ALU.add))
                        chain(nc.vector.bn_stats(stats[:, :], resd))
                        if l == 0:
                            nc.vector.tensor_copy(mv[0][:, 2:3], psZ[:, D:C]).then_inc(S["read"], 1)
                        else:
                            nc.vector.tensor_copy(mv[0][:, 2:3], stats[:, 0:1])
                        chain(nc.vector.bn_aggr(mv[0][:, 0:2], stats[:, :]))
                        nc.vector.tensor_scalar_add(mv[0][:, 1:2], mv[0][:, 1:2], EPS).then_inc(S["var"], 1)
                        dve.wait_ge(S["std"], t + 1)
                        chain(nc.vector.reciprocal(rs[0][:, :], sq[0][:, :]))
                        if l == 0:
                            dve.wait_ge(d_x1st[b], 16 * k)
                            dve.wait_ge(d_yst[b], 16 * k)
                            nc.vector.tensor_copy(dinv[:, bass.ds(t, 1)], rs[0][:, 1:2])
                            chain(nc.vector.tensor_scalar(x1d[b], resd, mv[0][:, 0:1], rs[0][:, 0:1],
                                                          ALU.subtract, ALU.mult))
                            nc.vector.tensor_scalar(y[b][:, :], x1d[b], rs[0][:, 1:2], None, ALU.mult
                                                    ).then_inc(S["tile"][b], 1)
                        else:
                            dve.wait_ge(d_ost[b], 16 * k)
                            nc.vector.tensor_scalar(x1d[b], resd, mv[0][:, 0:1], rs[0][:, 0:1],
                                                    ALU.subtract, ALU.mult).then_inc(S["tile"][b], 1)

                    tiles(dve, tile)



_INS = ['x', 'adj', 'L0_gnn_item_feat', 'L0_gnn_W_item', 'L0_gnn_b_item', 'L0_gnn_W_user', 'L0_gnn_b_user', 'L1_gnn_W']
_OUTS = [((10000, 128), 'float32')]


def kernel(**inputs):
    import numpy as _np
    import concourse.bacc as _bacc
    from concourse import mybir as _mybir
    from concourse.bass_utils import run_bass_kernel_spmd as _run

    nc = _bacc.Bacc("TRN2", target_bir_lowering=False, num_devices=1)
    arrays, args = {}, []
    for name in _INS:
        a = _np.ascontiguousarray(inputs[name])
        arrays[f"in_{name}_dram"] = a
        args.append(nc.dram_tensor(f"in_{name}_dram", a.shape, _mybir.dt.from_np(a.dtype), kind="ExternalInput").ap())
    for i, (shape, dtype) in enumerate(_OUTS):
        dt = _mybir.dt.from_np(_np.dtype(dtype))
        args.append(nc.dram_tensor(f"out_{i}_dram", shape, dt, kind="ExternalOutput").ap())
    gnn_kernel(nc, *args)
    r = _run(nc, [arrays], core_ids=[0])
    return r.results[0]["out_0_dram"]
```

```python
from contextlib import ExitStack

import concourse.bass as bass
from concourse import mybir

P = 128
F32 = mybir.dt.float32
BF16 = mybir.dt.bfloat16
U32 = mybir.dt.uint32
I32 = mybir.dt.int32
ALU = mybir.AluOpType
ACT = mybir.ActivationFunctionType
AX_X = mybir.AxisListType.X
EPS = 1e-5

GROUP = 4
NB = 20
PIECES = 4
SLOTS = 16
CH = 3
RING = 4
LAG = 7
LAG2 = 7
EXP_MASK = 0x7F800000
LOW = -1.0e9


def gnn_kernel(nc, x, adj, item, W_item, b_item, W_user, b_user, W1, out):
    N, D = x.shape
    assert D == P
    NT = -(-N // P)
    TAIL0 = N - P
    NFULL = N // P
    REST = N - NFULL * P
    PAIRS = (NT - 1) // 2
    assert NT == 2 * PAIRS + 1 and 0 < REST
    C = D + 1
    CW = N // NB
    HALF = CW // 2
    BPP = NB // PIECES
    PW = N // PIECES
    NE = CH * P
    OWN = (CH - 1) * P
    GROUPS = -(-NT // GROUP)
    RING2 = 2 * GROUP
    NF = 2 + SLOTS
    assert CW * NB == N and NB % PIECES == 0 and NB <= 24 and CW <= 512

    x1_dram = nc.dram_tensor("x1_scratch", (N, D), F32, kind="Internal").ap()
    y_dram = nc.dram_tensor("y_scratch", (N, D), F32, kind="Internal").ap()
    adj_flat = adj.rearrange("a (b o) -> (a b) o", o=1)

    with ExitStack() as ctx:
        def sb(name, shape, dt=F32):
            return ctx.enter_context(nc.sbuf_tensor(name, shape, dt))

        def ps(name, shape, dt=F32):
            return ctx.enter_context(nc.psum_tensor(name, shape, dt))

        def sem(name):
            return ctx.enter_context(nc.semaphore(name))

        adj_rows = [sb(f"adj_rows{b}", [P, N]) for b in range(2)]
        feat = sb("feat", [P, NT, C])
        xall = feat[:, :, 0:D]
        signs = [sb(f"signs{p}", [P, PW], BF16) for p in range(PIECES)]
        sgn = [sb(f"sgn{b}", [P, PIECES]) for b in range(2)]
        pow2 = sb("pow2", [P, NB, P], BF16)
        ident = sb("ident", [P, P])
        before = sb("before", [P, P])
        shift = sb("shift", [P, P])
        delta = sb("delta", [P, P])
        iota_i = sb("iota_i", [P, NE], I32)
        iota_e = sb("iota_e", [P, NE])
        entry_no = sb("entry_no", [P, CH])
        halves = sb("halves", [P, SLOTS])
        top = [sb(f"top{b}", [P, SLOTS]) for b in range(2)]
        cidx = sb("cidx", [P, SLOTS], U32)
        cbase = sb("cbase", [P, SLOTS])
        masks3 = sb("masks3", [P, 3, SLOTS])
        high = sb("high", [P, SLOTS])
        expo = sb("expo", [P, 3, SLOTS], I32)
        keys = sb("keys", [P, 3, SLOTS])
        keys2 = sb("keys2", [P, 3, SLOTS])
        picked = sb("picked", [P, SLOTS])
        junk16 = sb("junk16", [P, SLOTS])
        rowcodes = [sb(f"rowcodes{b}", [P, 1 + SLOTS]) for b in range(2)]
        lowest = sb("lowest", [P, 1])
        sgnsum = sb("sgnsum", [P, 1])
        bad = sb("bad", [P, 1])
        most = sb("most", [P, 1])
        steps_m = sb("steps_m", [P, NE])
        fields = [sb(f"fields{b}", [P, NF]) for b in range(2)]
        slot = sb("slot", [P, CH])
        hit = sb("hit", [P, CH, SLOTS])
        code = sb("code", [P, CH])
        col = sb("col", [P, CH])
        jix = [sb(f"jix{b}", [P, CH], U32) for b in range(RING)]
        rel = [sb(f"rel{b}", [P, CH], U32) for b in range(RING)]
        vix = [sb(f"vix{b}", [P, CH], U32) for b in range(RING)]
        tile_base = [sb(f"tile_base{b}", [P, CH], U32) for b in range(RING)]
        ring_step = sb("ring_step", [P, CH], U32)
        jall = sb("jall", [P, GROUPS * GROUP * CH])
        jshared = sb("jshared", [P, GROUPS])
        jixs = [sb(f"jixs{b}", [P, 1], U32) for b in range(2)]
        Gs = [sb(f"Gs{b}", [P, P]) for b in range(2)]
        ones_m = sb("ones_m", [P, P])
        spill = [sb(f"spill{b}", [P, 1]) for b in range(GROUP + 1)]
        over = sb("over", [P, 1])
        entry_pos = sb("entry_pos", [P, CH])
        rall = sb("rall", [P, NT * CH])
        vall = sb("vall", [P, NT * CH])
        valid = sb("valid", [P, NT * CH])
        vraw = [sb(f"vraw{b}", [P, CH]) for b in range(RING)]
        G = [sb(f"G{b}", [P, CH + 1, P]) for b in range(RING)]
        M = [sb(f"M{b}", [P, CH + 1, P]) for b in range(2)]
        diag = sb("diag", [P, NT])
        row_key = sb("row_key", [P, NT])
        all_found = sb("all_found", [P, 1])
        listed = sb("listed", [P, 1])
        junk48 = sb("junk48", [P, 3, SLOTS])
        xs = sb("xs", [P, D])
        xT = sb("xT", [P, P])
        aggT = sb("aggT", [P, P])
        rs2 = sb("rs2", [2, P])
        bias2 = sb("bias2", [2, C])
        ones_col = sb("ones_col", [P, 1])
        w_raw = sb("w_raw", [P, 2, D])
        WiT = sb("WiT", [P, D])
        WuT = sb("WuT", [P, D])
        W1sb = sb("W1sb", [P, D])
        dinv = sb("dinv", [P, NT])
        stats = sb("stats", [P, 6])
        mv = [sb(f"mv{b}", [P, 3]) for b in range(2)]
        sq = [sb(f"sq{b}", [P, 2]) for b in range(2)]
        rs = [sb(f"rs{b}", [P, 2]) for b in range(2)]
        y = [sb(f"y{b}", [P, D]) for b in range(2)]
        zs = sb("zs", [P, D])
        res = [sb(f"res{b}", [P, D]) for b in range(2)]
        flag = sb("flag", [1, 1], I32)

        bank = [ps(f"bank{n}", [P, 512]) for n in range(8)]
        psM = bank[0:2]
        psS, psF, psA, psX, psZ, psW = bank[2:8]
        psA2, psZ2 = [psA, psX], [psZ, psW]
        aggT2 = [aggT, xT]
        psF4 = psF[:, 0:CH * NF].rearrange("p (q f) -> p q f", f=NF)

        s_zero = sem("zeros_set")
        s_const = sem("constants_made")
        s_cst2 = sem("derived_constants_made")
        s_w = sem("weights_landed")
        s_x = sem("x_landed")
        s_wT = sem("weights_transposed")
        s_wTc = sem("weightsT_copied")
        s_adj = [[sem(f"adj_landed{b}{p}") for p in range(PIECES)] for b in range(2)]
        s_sign = [sem(f"signs_written{p}") for p in range(PIECES)]
        s_fold = [sem(f"signs_folded{p}") for p in range(PIECES)]
        s_mread = [sem(f"masks_read{b}") for b in range(2)]
        s_find = sem("find_steps")
        s_codes = sem("row_codes_ready")
        s_small = sem("offsets_ready")
        s_ent = sem("entry_steps")
        s_steps = sem("row_steps_ready")
        s_fld = sem("entry_fields_ready")
        s_idx = sem("indices_ready")
        s_last = sem("last_tile_rows_bounded")
        s_vix = sem("value_indices_ready")
        s_vg = [sem(f"values_gathered{b}") for b in range(RING)]
        s_G = [sem(f"rows_gathered{b}") for b in range(RING)]
        s_own = [sem(f"own_rows_landed{b}") for b in range(RING)]
        s_diag = sem("diagonal_landed")
        s_val = sem("values_masked")
        s_M = sem("scatter_ready")
        s_xs = sem("x_tile_copied")
        s_xt = sem("x_transposed")
        s_xTc = sem("xT_copied")
        s_agg = sem("aggregate_ready")
        s_aggc = sem("aggregate_copied")
        s_z = sem("z_ready")
        s_ep1 = sem("residual_steps")
        s_var = sem("variance_ready")
        s_std = sem("std_ready")
        s_ep2 = sem("norm_steps")
        s_y = [sem(f"y_ready{b}") for b in range(2)]
        s_yst = [sem(f"y_stored{b}") for b in range(2)]
        s_fin2 = sem("norm_chain")
        s_fin = sem("flag_steps")
        s_flagp = sem("flag_summed")
        s_flag = sem("flag_ready")

        s2_turn = sem("gather2_turns")
        s2_jix = sem("list_indices_copied")
        s2_G = [sem(f"y_rows_gathered{b}") for b in range(RING)]
        s2_own = [sem(f"own_y_rows_landed{b}") for b in range(RING)]
        s2_Gs = [sem(f"shared_y_rows_gathered{b}") for b in range(2)]
        s2_prep = sem("shared_indices_summed")
        s2_diag = sem("scatter2_diagonal_ready")
        s2_M = sem("scatter2_ready")
        s2_agg = sem("aggregate2_ready")
        s2_aggc = sem("aggregate2_copied")
        s2_z = sem("z2_ready")
        s2_ep1 = sem("residual2_steps")
        s2_var = sem("variance2_ready")
        s2_std = sem("std2_ready")
        s2_n = sem("norm2_steps")
        s2_o = [sem(f"out_ready{b}") for b in range(2)]
        s2_ost = [sem(f"out_stored{b}") for b in range(2)]

        GB = 4
        widths = [P] * NFULL + [REST]
        groups = [list(range(g, min(g + GB, NT))) for g in range(0, NT, GB)]
        NG = len(groups)
        assert NG % 2 == 0
        HG = NG // 2
        assert CH + 1 == GB
        blkT = [G[b][:, :, :].rearrange("p a b -> p (a b)") for b in range(2)]
        xin = [M[b][:, 0, :] for b in range(2)]
        resd = M[0][:, 1, :]
        x1d = [M[b][:, 2, :] for b in range(2)]
        pick = sb("pick", [2, 2, P])
        d_sel = sem("d_pick_made")
        d_ones = sem("d_ones_set")
        d_item = sem("d_item_landed")
        d_it = sem("d_item_transposed")
        d_itc = sem("d_itemT_copied")
        d_h = sem("d_h_computed")
        d_hc = sem("d_h_copied")
        d_y2 = sem("d_y_landed")
        d_yst = [sem(f"d_y_stored{b}") for b in range(2)]
        d_x1st = [sem(f"d_x1_stored{b}") for b in range(2)]
        d_ost = [sem(f"d_out_stored{b}") for b in range(2)]
        L = [dict(
            adj=[sem(f"d_adj_landed{l}{b}") for b in range(2)],
            xin=[sem(f"d_x_landed{l}{b}") for b in range(2)],
            tr=[sem(f"d_transposed{l}{b}") for b in range(2)],
            cp=[sem(f"d_copied{l}{b}") for b in range(2)],
            mm=[sem(f"d_multiplied{l}{b}") for b in range(2)],
            xt=sem(f"d_x_transposed{l}"),
            xtc=sem(f"d_xT_copied{l}"),
            acc=sem(f"d_sum_ready{l}"),
            read=sem(f"d_sum_read{l}"),
            zm=sem(f"d_z_multiplied{l}"),
            steps=sem(f"d_vector_steps{l}"),
            var=sem(f"d_variance_ready{l}"),
            std=sem(f"d_std_ready{l}"),
            tile=[sem(f"d_tile_done{l}{b}") for b in range(2)],
        ) for l in range(2)]

        def tiles(eng, body):
            for b in range(2):
                body(b, 0, b, b * P)
            with eng.Fori(1, PAIRS) as k:
                for b in range(2):
                    body(2 * k + b, k, b, k * (2 * P) + b * P)
            body(NT - 1, PAIRS, 0, TAIL0)

        def stage(k, b, lag):
            kk = k + (b - lag) // RING
            pp = (b - lag) % RING
            return RING * kk + pp, kk, pp, 2 * kk + pp // 2, pp % 2

        def height(t):
            return REST if isinstance(t, int) and t == NT - 1 else P

        def rows(t):
            return bass.ds(t * P, height(t))

        def live(t):
            return not isinstance(t, int) or 0 <= t < NT

        def stage2(k, b, lag):
            kk = k + (b - lag) // RING2
            p = (b - lag) % RING2
            return RING2 * kk + p, 2 * kk + p // RING, p % RING, 4 * kk + p // 2, p % 2, kk, p // GROUP

        def iterations(eng, body, lag, ring=RING):
            head = -(-lag // ring)
            for i in range(head * ring):
                body(i // ring, i % ring)
            with eng.Fori(head, NT // ring) as k:
                for b in range(ring):
                    body(k, b)
            for i in range(NT // ring * ring, NT + lag):
                body(i // ring, i % ring)

        NZERO = 11 + RING
        NCONST = 6
        NCST2 = 4

        block = ctx.enter_context(nc.Block())

        @block.sync
        def _(sp):
            def load(k, b, r0, n=P):
                for p in range(PIECES):
                    sp.wait_ge(s_sign[p], 2 * k + b - 1 if not isinstance(k, int) or k else 0)
                    sp.dma_start(adj_rows[b][0:n, p * PW:(p + 1) * PW],
                                 adj[bass.ds(r0, n), p * PW:(p + 1) * PW]).then_inc(s_adj[b][p], 16)

            load(0, 0, 0)
            sp.dma_start(w_raw[:, 0, :], W_item).then_inc(s_w, 16)
            sp.dma_start(w_raw[:, 1, :], W_user).then_inc(s_w, 16)
            sp.dma_start(W1sb[:, :], W1).then_inc(s_w, 16)
            sp.wait_ge(s_const, NCONST)
            sp.dma_start(bias2[0:1, 0:D], b_item.rearrange("(a n) -> a n", a=1)).then_inc(s_w, 16)
            sp.dma_start(bias2[1:2, 0:D], b_user.rearrange("(a n) -> a n", a=1)).then_inc(s_w, 16)
            load(0, 1, P)
            sp.dma_start(xall[:, 0:NFULL, :],
                         x[0:NFULL * P, :].rearrange("(b p) d -> p b d", p=P)).then_inc(s_x, 16)
            sp.dma_start(xall[0:REST, NFULL, :], x[NFULL * P:N, :]).then_inc(s_x, 16)
            with sp.Fori(1, PAIRS) as k:
                for b in range(2):
                    load(k, b, k * (2 * P) + b * P)
            load(PAIRS, 0, NFULL * P, REST)

            sp.wait_ge(s_flag, 1)
            faults = sp.value_load(flag[0:1, 0:1], min_val=0, max_val=1 << 20)
            with sp.If(faults == 0):
                sp.wait_ge(s_yst[0], 16 * (PAIRS + 1))
                sp.wait_ge(s_yst[1], 16 * PAIRS)

                def own_y(k, b):
                    t, kk, pp = stage2(k, b, 0)[0:3]
                    if live(t):
                        sp.wait_ge(s2_agg, t - (RING - 1) if not isinstance(t, int) else max(t - (RING - 1), 0))
                        sp.dma_start(G[pp][0:height(t), CH, :], y_dram[rows(t), :]).then_inc(s2_own[pp], 16)

                iterations(sp, own_y, LAG2, RING2)
            with sp.Else():
                iv = adj_rows[1][:, 0:NFULL * D].rearrange("p (b d) -> p b d", d=D)
                sp.dma_start(iv, item[0:NFULL * P, :].rearrange("(b p) d -> p b d", p=P)).then_inc(d_item, 16)
                sp.dma_start(adj_rows[0][0:REST, 0:D], item[NFULL * P:N, :]).then_inc(d_item, 16)

                for l in range(2):
                    S = L[l]
                    if l == 0:
                        sp.wait_ge(d_it, NT)
                    else:
                        for b, n in ((0, PAIRS + 1), (1, PAIRS)):
                            sp.wait_ge(d_yst[b], 16 * n)
                            sp.wait_ge(d_x1st[b], 16 * n)
                        sp.dma_start(feat[:, 0:NFULL, 0:D],
                                     y_dram[0:NFULL * P, :].rearrange("(b p) d -> p b d", p=P)).then_inc(d_y2, 16)
                        sp.dma_start(feat[0:REST, NFULL, 0:D], y_dram[NFULL * P:N, :]).then_inc(d_y2, 16)

                    def tile(t, k, b, r0):
                        sp.wait_ge(S["tile"][b], k)
                        sp.dma_start(adj_rows[b][:, :], adj[bass.ds(r0, P), :]).then_inc(S["adj"][b], 16)
                        src = x if l == 0 else x1_dram
                        sp.dma_start(xin[b], src[bass.ds(r0, P), :]).then_inc(S["xin"][b], 16)

                    tiles(sp, tile)


        @block.gpsimd
        def _(pool):
            pool.memset(ident[:, :], 0.0).then_inc(s_zero, 1)
            pool.memset(shift[:, :], 0.0).then_inc(s_zero, 1)
            pool.memset(before[:, :], 1.0).then_inc(s_zero, 1)
            pool.memset(ones_col[:, :], 1.0).then_inc(s_zero, 1)
            pool.memset(ones_m[:, :], 1.0).then_inc(s_zero, 1)
            pool.memset(diag[:, NFULL:NT], 1.0).then_inc(s_zero, 1)
            pool.memset(xall[:, NFULL, :], 0.0).then_inc(s_zero, 1)
            pool.memset(rs2[:, :], 1.0).then_inc(s_zero, 1)
            pool.memset(bias2[:, :], 0.0).then_inc(s_zero, 1)
            pool.memset(ring_step[:, :], RING * P * N).then_inc(s_zero, 1)
            for b in range(RING):
                pool.memset(tile_base[b][:, :], b * P * N).then_inc(s_zero, 1)
            pool.iota(iota_i[:, :], [[1, NE]], base=0, channel_multiplier=0).then_inc(s_zero, 1)
            pool.wait_ge(s_zero, NZERO)
            pool.affine_select(out=ident[:, :], in_=ident[:, :], compare_op=ALU.not_equal, fill=1.0,
                               base=0, pattern=[[-1, P]], channel_multiplier=1).then_inc(s_const, 1)
            pool.affine_select(out=shift[:, :], in_=shift[:, :], compare_op=ALU.not_equal, fill=1.0,
                               base=1, pattern=[[-1, P]], channel_multiplier=1).then_inc(s_const, 1)
            pool.affine_select(out=before[:, :], in_=before[:, :], compare_op=ALU.is_gt, fill=0.0,
                               base=0, pattern=[[1, P]], channel_multiplier=-1).then_inc(s_const, 1)
            pool.memset(bias2[0:1, D:C], 1.0).then_inc(s_const, 1)
            pool.iota(entry_no[:, :], [[P, CH]], base=0, channel_multiplier=1,
                      allow_small_or_imprecise_dtypes=True).then_inc(s_const, 1)
            pool.iota(row_key[:, :], [[P, NT]], base=1, channel_multiplier=1,
                      allow_small_or_imprecise_dtypes=True).then_inc(s_const, 1)

            def gather(k, b):
                t, kk, pp, c2, p2 = stage(k, b, 2)
                if live(t):
                    pool.wait_ge(s_val, t - (RING - 1) if not isinstance(t, int) else max(t - (RING - 1), 0))
                    pool.wait_ge(s_idx, t + 1)
                    pool.tensor_tensor(vix[pp][:, :], rel[pp][:, :], tile_base[pp][:, :], ALU.add).then_inc(s_vix, 1)
                    pool.wait_ge(s_vix, 2 * t + 1)
                    pool.wait_ge(s_agg, t - (RING - 1) if not isinstance(t, int) else max(t - (RING - 1), 0))
                    pool.tensor_tensor(tile_base[pp][:, :], tile_base[pp][:, :], ring_step[:, :],
                                       ALU.add).then_inc(s_vix, 1)
                    for q in range(CH):
                        pool.indirect_dma_start(vraw[pp][:, q:q + 1], None, adj_flat,
                                                bass.IndirectOffsetOnAxis(ap=vix[pp][:, q:q + 1], axis=0)
                                                ).then_inc(s_vg[pp], 16)
                    for q in range(CH):
                        pool.indirect_dma_start(G[pp][:, q, :], None, item,
                                                bass.IndirectOffsetOnAxis(ap=jix[pp][:, q:q + 1], axis=0)
                                                ).then_inc(s_G[pp], 16)

            iterations(pool, gather, LAG)

            pool.wait_ge(s_flag, 1)
            faults = pool.value_load(flag[0:1, 0:1], min_val=0, max_val=1 << 20)
            with pool.If(faults == 0):
                pool.wait_ge(s_yst[0], 16 * (PAIRS + 1))
                pool.wait_ge(s_yst[1], 16 * PAIRS)

                def gather_y(k, b):
                    t, _, pp, _, _, _, g2 = stage2(k, b, 0)
                    if live(t):
                        pool.wait_ge(s2_agg, t - (RING - 1) if not isinstance(t, int) else max(t - (RING - 1), 0))
                        pool.wait_ge(s2_jix, t + 1)
                        pool.wait_ge(s2_turn, t)
                        pool.tensor_tensor(vix[pp][:, :], ring_step[:, :], ring_step[:, :], ALU.add).then_inc(s2_turn, 1)
                        if pp == 0:
                            pool.indirect_dma_start(Gs[g2][:, :], None, y_dram,
                                                    bass.IndirectOffsetOnAxis(ap=jixs[g2][:, 0:1], axis=0)
                                                    ).then_inc(s2_Gs[g2], 16)
                        for q in range(CH - 1):
                            pool.indirect_dma_start(G[pp][:, q, :], None, y_dram,
                                                    bass.IndirectOffsetOnAxis(ap=jix[pp][:, q:q + 1], axis=0)
                                                    ).then_inc(s2_G[pp], 16)

                iterations(pool, gather_y, LAG2, RING2)
            with pool.Else():
                pool.wait_ge(s_yst[0], 16 * (PAIRS + 1))
                pool.wait_ge(s_yst[1], 16 * PAIRS)
                pool.memset(feat[:, :, D:C], 1.0).then_inc(d_ones, 1)

                def store1(t, k, b, r0):
                    pool.wait_ge(L[0]["tile"][b], k + 1)
                    if r0 is TAIL0:
                        pool.wait_ge(d_x1st[1], 16 * PAIRS)
                        pool.wait_ge(d_yst[1], 16 * PAIRS)
                    pool.dma_start(x1_dram[bass.ds(r0, P), :], x1d[b]).then_inc(d_x1st[b], 16)
                    pool.dma_start(y_dram[bass.ds(r0, P), :], y[b][:, :]).then_inc(d_yst[b], 16)

                tiles(pool, store1)

                def store2(t, k, b, r0):
                    pool.wait_ge(L[1]["tile"][b], k + 1)
                    if r0 is TAIL0:
                        pool.wait_ge(d_ost[1], 16 * PAIRS)
                    pool.dma_start(out[bass.ds(r0, P), :], x1d[b]).then_inc(d_ost[b], 16)

                tiles(pool, store2)
                pool.wait_ge(d_ost[0], 16 * (PAIRS + 1))
                pool.wait_ge(d_ost[1], 16 * PAIRS)


        @block.tensor
        def _(pe):
            pe.wait_ge(s_w, 80)
            pe.wait_ge(s_const, NCONST)
            for i, ps_w in enumerate((psX, psZ)):
                nc.tensor.transpose(ps_w[:, 0:P], w_raw[:, i, :], ident[:, :]).then_inc(s_wT, 1)
            pe.wait_ge(s_wTc, 2)
            pe.wait_ge(s_cst2, NCST2)

            def fold(t, pp, pieces):
                n = height(t)
                for p in pieces:
                    pe.wait_ge(s_sign[p], t + 1)
                    for j in range(BPP):
                        blk = p * BPP + j
                        last = nc.tensor.matmul(psM[pp][:, 0:CW], pow2[0:n, blk, :], signs[p][0:n, j * CW:(j + 1) * CW],
                                                start=(blk == 0), stop=(blk == NB - 1))
                    last.then_inc(s_fold[p], 1)

            def body(k, b):
                t0, _, _, k0, p0 = stage(k, b, 0)
                t2, _, _, _, p2_2 = stage(k, b, 2)
                t, kk, pp, c2, p2 = stage(k, b, 5)
                if live(t2):
                    pe.wait_ge(s_codes, t2 + 1)
                    nc.tensor.matmul(psS[:, 0:1], before[:, :], rowcodes[p2_2][:, 0:1], start=True, stop=True)
                    nc.tensor.matmul(psS[:, 1:2], shift[:, :], rowcodes[p2_2][:, 0:1], start=True, stop=True)
                    nc.tensor.matmul(psS[:, NF:NF + 1], ones_m[:, :], rowcodes[p2_2][:, 0:1], start=True, stop=True)
                    nc.tensor.matmul(psS[:, 2:NF], delta[:, :], rowcodes[p2_2][:, 1:1 + SLOTS],
                                     start=True, stop=True).then_inc(s_small, 1)
                if live(t0):
                    pe.wait_ge(s_mread[p0], k0)
                    fold(t0, p0, (0, 1))
                if live(t2):
                    pe.wait_ge(s_steps, t2 + 1)
                    for q in range(CH):
                        last = nc.tensor.matmul(psF4[:, q, :], steps_m[:, q * P:(q + 1) * P], fields[p2_2][:, :],
                                                start=True, stop=True)
                    last.then_inc(s_fld, 1)
                if live(t):
                    pe.wait_ge(s_xs, t + 1)
                    nc.tensor.transpose(psX[:, 0:P], xs[:, :], ident[:, :]).then_inc(s_xt, 1)
                    pe.wait_ge(s_M, t + 1)
                    pe.wait_ge(s_own[pp], 16 * (kk + 1))
                    pe.wait_ge(s_G[pp], 16 * CH * (kk + 1))
                    for q in range(CH + 1):
                        nc.tensor.matmul(psA[:, 0:P], G[pp][:, q, :], M[p2][:, q, :],
                                         start=(q == 0), stop=(q == CH))
                    for q in range(CH + 1):
                        last = nc.tensor.matmul(psA[0:1, P:2 * P], ones_col[:, :], M[p2][:, q, :],
                                                start=(q == 0), stop=(q == CH))
                    last.then_inc(s_agg, 1)
                if live(t0):
                    fold(t0, p0, (2,))
                if live(t):
                    pe.wait_ge(s_aggc, t + 1)
                    pe.wait_ge(s_var, t)
                    nc.tensor.matmul(psZ[:, 0:C], rs2[:, :], bias2[:, :], start=True, stop=False)
                    nc.tensor.matmul(psZ[:, 0:D], xT[:, :], WuT[:, :], start=False, stop=False)
                    nc.tensor.matmul(psZ[:, 0:D], aggT[:, :], WiT[:, :], start=False, stop=True).then_inc(s_z, 1)
                if live(t0):
                    fold(t0, p0, (3,))

            iterations(pe, body, LAG)
            pe.wait_ge(s_fin, 1)
            nc.tensor.matmul(psS[0:1, 0:1], bad[:, :], ones_col[:, :], start=True, stop=True).then_inc(s_flagp, 1)

            pe.wait_ge(s_flag, 1)
            faults = pe.value_load(flag[0:1, 0:1], min_val=0, max_val=1 << 20)
            with pe.If(faults == 0):
                def body2(k, b):
                    t, kk, pp, c2, p2, kg, g2 = stage2(k, b, 4)
                    if live(t):
                        pe.wait_ge(s2_M, t + 1)
                        pe.wait_ge(s2_diag, t + 1)
                        pe.wait_ge(s2_G[pp], 16 * (CH - 1) * (kk + 1))
                        pe.wait_ge(s2_Gs[g2], 16 * (kg + 1))
                        pe.wait_ge(s2_own[pp], 16 * (kk + 1))
                        pe.wait_ge(s2_aggc, t - 1 if not isinstance(t, int) else max(t - 1, 0))
                        rows = [G[pp][:, q, :] for q in range(CH - 1)] + [Gs[g2][:, :], G[pp][:, CH, :]]
                        for q in range(CH + 1):
                            last = nc.tensor.matmul(psA2[p2][:, 0:P], rows[q], M[p2][:, q, :],
                                                    start=(q == 0), stop=(q == CH))
                        last.then_inc(s2_agg, 1)
                    t, kk, pp, c2, p2 = stage2(k, b, 5)[0:5]
                    if live(t):
                        pe.wait_ge(s2_aggc, t + 1)
                        pe.wait_ge(s2_var, t - 1 if not isinstance(t, int) else max(t - 1, 0))
                        nc.tensor.matmul(psZ2[p2][:, 0:D], aggT2[p2][:, :], W1sb[:, :],
                                         start=True, stop=True).then_inc(s2_z, 1)

                iterations(pe, body2, LAG2, RING2)
            with pe.Else():
                pe.wait_ge(d_ones, 1)
                pe.wait_ge(d_sel, 1)
                pe.wait_ge(d_item, 32)

                def h_block(b, src, w):
                    pe.wait_ge(d_itc, b)
                    nc.tensor.transpose(psM[0][:, 0:w], src, ident[0:w, 0:w]).then_inc(d_it, 1)
                    pe.wait_ge(d_itc, b + 1)
                    pe.wait_ge(d_hc, b)
                    nc.tensor.matmul(psZ[0:w, 0:D], xT[:, 0:w], WiT[:, :], start=True, stop=False)
                    nc.tensor.matmul(psZ[0:w, 0:D], pick[:, 0, 0:w], bias2[:, 0:D], start=False, stop=True).then_inc(d_h, 1)

                for b in range(NFULL):
                    h_block(b, adj_rows[1][:, b * D:(b + 1) * D], P)
                h_block(NFULL, adj_rows[0][0:REST, 0:D], REST)
                pe.wait_ge(d_hc, NT)

                for l in range(2):
                    S = L[l]
                    if l == 1:
                        pe.wait_ge(d_y2, 32)

                    def tile(t, k, b, r0):
                        pe.wait_ge(S["adj"][b], 16 * (k + 1))
                        if l == 0:
                            pe.wait_ge(S["xin"][b], 16 * (k + 1))
                            nc.tensor.transpose(psX[:, 0:P], xin[b], ident[:, :]).then_inc(S["xt"], 1)

                        def transposes(g):
                            e = g % 2
                            pe.wait_ge(S["cp"][e], t * HG + g // 2)
                            for i, c in enumerate(groups[g]):
                                w = widths[c]
                                last = nc.tensor.transpose(psM[e][0:w, i * P:(i + 1) * P],
                                                           adj_rows[b][:, c * P:c * P + w], ident[:, :])
                            last.then_inc(S["tr"][e], 1)

                        def products(g):
                            e = g % 2
                            pe.wait_ge(S["cp"][e], t * HG + g // 2 + 1)
                            if g == 0 and l == 0:
                                pe.wait_ge(S["read"], t)
                            for i, c in enumerate(groups[g]):
                                w = widths[c]
                                last = nc.tensor.matmul(psZ[:, 0:C], blkT[e][0:w, i * P:(i + 1) * P], feat[0:w, c, :],
                                                        start=(c == 0), stop=(l == 1 and c == NT - 1))
                            last.then_inc(S["mm"][e], 1)

                        transposes(0)
                        for g in range(NG):
                            if g + 1 < NG:
                                transposes(g + 1)
                            products(g)
                        if l == 0:
                            pe.wait_ge(S["xtc"], t + 1)
                            nc.tensor.matmul(psZ[:, 0:D], xT[:, :], WuT[:, :], start=False, stop=False)
                            nc.tensor.matmul(psZ[:, 0:D], pick[:, 1, :], bias2[:, 0:D], start=False, stop=True).then_inc(S["acc"], 1)
                        else:
                            pe.wait_ge(S["steps"], t * 5 + 1)
                            nc.tensor.transpose(psX[:, 0:P], zs[:, :], ident[:, :]).then_inc(S["xt"], 1)
                            pe.wait_ge(S["xtc"], t + 1)
                            nc.tensor.matmul(psW[:, 0:D], xT[:, :], W1sb[:, :], start=True, stop=True).then_inc(S["zm"], 1)

                    tiles(pe, tile)


        @block.scalar
        def _(act):
            def sign(t, k, b, pieces):
                n = height(t)
                for p in pieces:
                    act.wait_ge(s_adj[b][p], 16 * (k + 1))
                    if p == 0:
                        act.wait_ge(s_codes, t - 1 if not isinstance(t, int) else max(t - 1, 0))
                    act.wait_ge(s_fold[p], t)
                    nc.scalar.activation(signs[p][0:n, :], adj_rows[b][0:n, p * PW:(p + 1) * PW], ACT.Sign,
                                         accum_out=sgn[b][0:n, p:p + 1]).then_inc(s_sign[p], 1)

            diag_view = adj_flat[0:(NFULL * P - 1) * (N + 1) + 1:N + 1, :].rearrange("(t p) o -> p (t o)", p=P)
            act.dma_start(diag[:, 0:NFULL], diag_view, allow_slow_non_contiguous=True).then_inc(s_diag, 16)
            tail_view = adj_flat[NFULL * P * (N + 1):(N - 1) * (N + 1) + 1:N + 1, :]
            act.wait_ge(s_zero, NZERO)
            act.dma_start(diag[0:REST, NFULL:NT], tail_view, allow_slow_non_contiguous=True).then_inc(s_diag, 16)
            sign(0, 0, 0, range(PIECES))
            for i, (dst, ps_w) in enumerate(((WiT, psX), (WuT, psZ))):
                act.wait_ge(s_wT, i + 1)
                nc.scalar.copy(dst[:, :], ps_w[:, 0:P]).then_inc(s_wTc, 1)

            def body(k, b):
                t0, _, _, k0, p0 = stage(k, b, 0)
                first = isinstance(t0, int) and t0 == 0
                if live(t0) and not first:
                    sign(t0, k0, p0, (0, 1))
                t, kk, pp, c2, p2 = stage(k, b, 5)
                if live(t):
                    if isinstance(t, int) and t == 0:
                        act.wait_ge(s_x, 32)
                    act.wait_ge(s_wTc, 2)
                    act.wait_ge(s_xt, t)
                    nc.scalar.copy(xs[:, :], xall[:, t, :]).then_inc(s_xs, 1)
                if live(t0) and not first:
                    sign(t0, k0, p0, (2,))
                if live(t):
                    act.wait_ge(s_xt, t + 1)
                    act.wait_ge(s_z, t)
                    nc.scalar.copy(xT[:, :], psX[:, 0:P]).then_inc(s_xTc, 1)
                    act.wait_ge(s_agg, t + 1)
                    nc.scalar.copy(aggT[:, :], psA[:, 0:P])
                    nc.scalar.copy(rs2[0:1, :], psA[0:1, P:2 * P]).then_inc(s_aggc, 1)
                if live(t0) and not first:
                    sign(t0, k0, p0, (3,))
                t, kk, pp, c2, p2 = stage(k, b, 6)
                if live(t):
                    act.wait_ge(s_ep2, t - 1 if not isinstance(t, int) else max(t - 1, 0))
                    act.wait_ge(s_var, t + 1)
                    nc.scalar.activation(sq[p2][:, :], mv[p2][:, 1:3], ACT.Sqrt).then_inc(s_std, 1)
                t, kk, pp, c2, p2 = stage(k, b, 2)
                if live(t):
                    act.wait_ge(s_agg, t - (RING - 1) if not isinstance(t, int) else max(t - (RING - 1), 0))
                    act.dma_start(G[pp][0:height(t), CH, :], item[rows(t), :]).then_inc(s_own[pp], 16)
                t, kk, pp, c2, p2 = stage(k, b, 7)
                if live(t):
                    act.wait_ge(s_y[p2], c2 + 1)
                    act.dma_start(y_dram[rows(t), :], y[p2][0:height(t), :]).then_inc(s_yst[p2], 16)

            iterations(act, body, LAG)
            act.wait_ge(s_yst[0], 16 * (PAIRS + 1))
            act.wait_ge(s_yst[1], 16 * PAIRS)

            act.wait_ge(s_flag, 1)
            faults = act.value_load(flag[0:1, 0:1], min_val=0, max_val=1 << 20)
            with act.If(faults == 0):
                def body2(k, b):
                    t, kk, pp, c2, p2 = stage2(k, b, 2)[0:5]
                    if live(t):
                        act.wait_ge(s2_agg, t - 1 if not isinstance(t, int) else max(t - 1, 0))
                        nc.scalar.activation(M[p2][:, CH, :], ident[:, :], ACT.Copy,
                                             scale=diag[:, bass.ds(t, 1)]).then_inc(s2_diag, 1)
                    t, kk, pp, c2, p2 = stage2(k, b, 4)[0:5]
                    if live(t):
                        act.wait_ge(s2_z, t - 1 if not isinstance(t, int) else max(t - 1, 0))
                        act.wait_ge(s2_agg, t + 1)
                        nc.scalar.copy(aggT2[p2][:, :], psA2[p2][:, 0:P]).then_inc(s2_aggc, 1)
                    t, kk, pp, c2, p2 = stage2(k, b, 7)[0:5]
                    if live(t):
                        act.wait_ge(s2_o[p2], c2 + 1)
                        act.dma_start(out[rows(t), :], y[p2][0:height(t), :]).then_inc(s2_ost[p2], 16)
                    t, kk, pp, c2, p2 = stage2(k, b, 5)[0:5]
                    if live(t):
                        act.wait_ge(s2_n, t - 1 if not isinstance(t, int) else max(t - 1, 0))
                        act.wait_ge(s2_var, t + 1)
                        nc.scalar.activation(sq[p2][:, 0:1], mv[p2][:, 1:2], ACT.Sqrt).then_inc(s2_std, 1)

                iterations(act, body2, LAG2, RING2)
                act.wait_ge(s2_ost[0], 16 * (PAIRS + 1))
                act.wait_ge(s2_ost[1], 16 * PAIRS)
            with act.Else():
                for b in range(NT):
                    w = widths[b]
                    act.wait_ge(d_it, b + 1)
                    act.wait_ge(d_h, b)
                    nc.scalar.copy(xT[:, 0:w], psM[0][:, 0:w]).then_inc(d_itc, 1)

                for l in range(2):
                    S = L[l]

                    def tile(t, k, b, r0):
                        def copy_xT():
                            act.wait_ge(S["xt"], t + 1)
                            act.wait_ge(S["acc"] if l == 0 else S["zm"], t)
                            nc.scalar.copy(xT[:, :], psX[:, 0:P]).then_inc(S["xtc"], 1)

                        if l == 0:
                            copy_xT()
                        for g in range(0, NG, 2):
                            act.wait_ge(S["tr"][0], t * HG + g // 2 + 1)
                            act.wait_ge(S["mm"][0], t * HG + g // 2)
                            nc.scalar.copy(blkT[0], psM[0][:, :]).then_inc(S["cp"][0], 1)
                        if l == 1:
                            copy_xT()
                        act.wait_ge(S["var"], t + 1)
                        n = 2 if l == 0 else 1
                        nc.scalar.activation(sq[0][:, 0:n], mv[0][:, 1:1 + n], ACT.Sqrt).then_inc(S["std"], 1)

                    tiles(act, tile)


        @block.vector
        def _(dve):
            def linker(semaphore, base):
                n = [base]

                def link(ins):
                    ins.then_inc(semaphore, 1)
                    n[0] = n[0] + 1
                    dve.wait_ge(semaphore, n[0])
                return link

            dve.wait_ge(s_zero, NZERO)
            dve.wait_ge(s_const, NCONST)
            dve.wait_ge(s_diag, 32)
            nc.vector.memset(bad[:, :], 0.0)
            nc.vector.memset(most[:, :], 0.0)
            nc.vector.memset(spill[0][:, :], 0.0)
            nc.vector.memset(jall[:, NT * CH:], 0.0)
            nc.vector.tensor_copy(entry_pos[:, :], entry_no[:, :])
            nc.vector.memset(halves[:, 0:8], -float(127 * CW - 1))
            nc.vector.memset(halves[:, 8:16], -float(127 * CW - 1 - HALF))
            nc.vector.tensor_copy(iota_e[:, :], iota_i[:, :]).then_inc(s_cst2, 1)
            nc.vector.tensor_tensor(delta[:, :], ident[:, :], shift[:, :], ALU.subtract).then_inc(s_cst2, 1)
            for blk in range(NB):
                last = nc.vector.tensor_scalar(pow2[:, blk, :], ident[:, :], float(2 ** blk), None, ALU.mult)
            last.then_inc(s_cst2, 1)
            for b in range(2):
                last = nc.vector.tensor_scalar(fields[b][:, 0:1], entry_no[:, 0:1], 1.0, None, ALU.min)
            last.then_inc(s_cst2, 1)
            dve.wait_ge(s_cst2, NCST2)

            def find(t, kk, pp, c2, p2):
                link = linker(s_find, t * 16)
                n = height(t)
                m = psM[p2][:, 0:CW]
                dve.wait_ge(s_fold[PIECES - 1], t + 1)
                nc.vector.tensor_reduce(lowest[:, :], m, AX_X, ALU.min)
                nc.vector.max(top[p2][:, 0:8], m[:, 0:HALF])
                link(nc.vector.max(top[p2][:, 8:16], m[:, HALF:CW]))
                nc.vector.tensor_scalar(masks3[:, 0, :], top[p2][:, :], 0.0, None, ALU.max)
                nc.vector.max_index(cidx[:, 0:8], top[p2][:, 0:8], m[:, 0:HALF])
                nc.vector.max_index(cidx[:, 8:16], top[p2][:, 8:16], m[:, HALF:CW]).then_inc(s_mread[p2], 1)
                dve.wait_ge(s_mread[p2], c2 + 1)
                for lv in range(2):
                    link(nc.vector.tensor_scalar(high[:, :].bitcast(I32), masks3[:, lv, :].bitcast(I32), EXP_MASK,
                                                 None, ALU.bitwise_and))
                    link(nc.vector.tensor_tensor(masks3[:, lv + 1, :], masks3[:, lv, :], high[:, :], ALU.subtract))
                link(nc.vector.tensor_scalar(expo[:, :, :], masks3[:, :, :].bitcast(I32), 23, None,
                                             ALU.logical_shift_right))
                link(nc.vector.tensor_tensor(cbase[:, :], cidx[:, :], halves[:, :], ALU.add))
                link(nc.vector.scalar_tensor_tensor(out=keys[:, :, :], in0=expo[:, :, :], scalar=float(CW),
                                                    in1=cbase[:, :].unsqueeze(1).to_broadcast([P, 3, SLOTS]),
                                                    op0=ALU.mult, op1=ALU.add))
                link(nc.vector.tensor_scalar(junk48[:, :, :], keys[:, :, :], 0.0, None, ALU.is_gt, ALU.add,
                                             accum_out=all_found[:, :]))
                link(nc.vector.scalar_tensor_tensor(out=keys[:, :, :], in0=keys[:, :, :],
                                                    scalar=row_key[:, bass.ds(t, 1)], in1=keys[:, :, :],
                                                    op0=ALU.not_equal, op1=ALU.mult))
                nc.vector.tensor_reduce(sgnsum[:, :], sgn[p2][:, :], AX_X, ALU.add)
                link(nc.vector.max(picked[:, 0:8], keys[:, :, :]))
                nc.vector.tensor_scalar(rowcodes[p2][:, 1:9], picked[:, 0:8], 0.0, None, ALU.max)
                link(nc.vector.match_replace(keys2[:, :, :], picked[:, 0:8], keys[:, :, :], LOW))
                nc.vector.scalar_tensor_tensor(out=bad[:, :], in0=lowest[:, :], scalar=0.0, in1=bad[:, :],
                                               op0=ALU.is_lt, op1=ALU.add)
                link(nc.vector.max(picked[:, 8:16], keys2[:, :, :]))
                nc.vector.tensor_scalar(rowcodes[p2][:, 9:1 + SLOTS], picked[:, 8:16], 0.0, None, ALU.max)
                nc.vector.tensor_scalar(junk16[:, :], picked[:, :], 0.0, None, ALU.is_gt, ALU.add,
                                        accum_out=rowcodes[p2][:, 0:1]).then_inc(s_codes, 1)
                link(nc.vector.scalar_tensor_tensor(out=bad[0:n, :], in0=sgnsum[0:n, :], scalar=all_found[0:n, :],
                                                    in1=bad[0:n, :], op0=ALU.not_equal, op1=ALU.add))
                dve.wait_ge(s_codes, t + 1)
                link(nc.vector.scalar_tensor_tensor(out=listed[:, :], in0=diag[:, bass.ds(t, 1)], scalar=0.0,
                                                    in1=rowcodes[p2][:, 0:1], op0=ALU.is_gt, op1=ALU.add))
                link(nc.vector.scalar_tensor_tensor(out=bad[0:n, :], in0=listed[0:n, :], scalar=all_found[0:n, :],
                                                    in1=bad[0:n, :], op0=ALU.not_equal, op1=ALU.add))

            def scatter(t, kk, pp, c2, p2):
                dve.wait_ge(s_vg[pp], 16 * CH * (kk + 1))
                nc.vector.tensor_tensor(vall[:, bass.ds(t * CH, CH)], vraw[pp][:, :],
                                        valid[:, bass.ds(t * CH, CH)], ALU.mult).then_inc(s_val, 1)
                dve.wait_ge(s_val, t + 1)
                dve.wait_ge(s_agg, t - 1 if not isinstance(t, int) else max(t - 1, 0))
                nc.vector.tensor_scalar(M[p2][:, CH, :], ident[:, :], diag[:, bass.ds(t, 1)], None, ALU.mult)
                for q in range(CH):
                    last = nc.vector.tensor_scalar(M[p2][:, q, :], iota_e[:, 0:P], rall[:, bass.ds(t * CH + q, 1)],
                                                   vall[:, bass.ds(t * CH + q, 1)], ALU.is_equal, ALU.mult)
                last.then_inc(s_M, 1)

            def row_steps(t, kk, pp, c2, p2):
                link = linker(s_ent, t * 10)
                dve.wait_ge(s_small, t + 1)
                dve.wait_ge(s_fld, t)
                nc.vector.tensor_copy(fields[p2][:, 1:NF], psS[:, 1:NF])
                nc.vector.tensor_scalar(steps_m[:, 0:OWN], iota_e[:, 0:OWN], psS[:, 0:1], None, ALU.is_ge)
                nc.vector.tensor_scalar(steps_m[:, OWN:NE], iota_e[:, OWN:NE], spill[pp][:, :], psS[:, 0:1],
                                        ALU.subtract, ALU.is_ge).then_inc(s_steps, 1)
                nc.vector.tensor_scalar(entry_pos[:, CH - 1:CH], entry_no[:, CH - 1:CH], spill[pp][:, :], None,
                                        ALU.subtract)
                link(nc.vector.tensor_scalar(over[:, :], psS[:, NF:NF + 1], -float(OWN), 0.0, ALU.add, ALU.max))
                link(nc.vector.tensor_tensor(spill[pp + 1][:, :], spill[pp][:, :], over[:, :], ALU.add))
                link(nc.vector.tensor_tensor(most[:, :], most[:, :], spill[pp + 1][:, :], ALU.max))

            def entries(t, kk, pp, c2, p2):
                link = linker(s_ent, t * 10 + 3)
                dve.wait_ge(s_fld, t + 1)
                link(nc.vector.tensor_tensor(slot[:, :], entry_pos[:, :], psF4[:, :, 1], ALU.subtract))
                link(nc.vector.tensor_tensor(hit[:, :, :], slot[:, :].unsqueeze(2).to_broadcast([P, CH, SLOTS]),
                                             iota_e[:, 0:SLOTS].unsqueeze(1).to_broadcast([P, CH, SLOTS]),
                                             ALU.is_equal))
                link(nc.vector.tensor_tensor(hit[:, :, :], hit[:, :, :], psF4[:, :, 2:NF], ALU.mult))
                link(nc.vector.tensor_reduce(code[:, :], hit[:, :, :], AX_X, ALU.add))
                link(nc.vector.scalar_tensor_tensor(out=code[:, CH - 1:CH], in0=entry_pos[:, CH - 1:CH],
                                                    scalar=float(OWN), in1=code[:, CH - 1:CH],
                                                    op0=ALU.is_ge, op1=ALU.mult))
                link(nc.vector.tensor_scalar(col[:, :], code[:, :], -1.0, 0.0, ALU.add, ALU.max))
                nc.vector.tensor_scalar(valid[:, bass.ds(t * CH, CH)], code[:, :], 1.0, None, ALU.min)
                nc.vector.tensor_copy(rall[:, bass.ds(t * CH, CH)], psF4[:, :, 0])
                nc.vector.tensor_copy(jall[:, bass.ds(t * CH, CH)], col[:, :])
                dve.wait_ge(s_G[pp], 16 * CH * kk)
                link(nc.vector.tensor_copy(jix[pp][:, :], col[:, :]))
                entry_row = psF4[:, :, 0]
                if height(t) < P:
                    dve.wait_ge(s_ent, t * 10 + 10)
                    entry_row = code[:, :]
                    nc.vector.tensor_scalar(code[:, :], psF4[:, :, 0], float(REST - 1), None,
                                            ALU.min).then_inc(s_last, 1)
                    dve.wait_ge(s_last, 1)
                nc.vector.scalar_tensor_tensor(out=rel[pp][:, :], in0=entry_row, scalar=float(N),
                                               in1=col[:, :], op0=ALU.mult, op1=ALU.add).then_inc(s_idx, 1)
                dve.wait_ge(s_idx, t + 1)

            def residual(t, kk, pp, c2, p2):
                link = linker(s_ep1, t * 3)
                dve.wait_ge(s_z, t + 1)
                link(nc.vector.scalar_tensor_tensor(out=res[p2][:, :], in0=psZ[:, 0:D], scalar=0.0,
                                                    in1=xall[:, t, :], op0=ALU.max, op1=ALU.add))
                link(nc.vector.bn_stats(stats[:, :], res[p2][:, :]))
                nc.vector.tensor_copy(mv[p2][:, 2:3], psZ[:, D:C])
                link(nc.vector.bn_aggr(mv[p2][:, 0:2], stats[:, :]))
                nc.vector.tensor_scalar_add(mv[p2][:, 1:2], mv[p2][:, 1:2], EPS).then_inc(s_var, 1)

            def norm(t, kk, pp, c2, p2):
                link = linker(s_fin2, t * 2)
                dve.wait_ge(s_std, t + 1)
                link(nc.vector.reciprocal(rs[p2][:, :], sq[p2][:, :]))
                nc.vector.tensor_copy(dinv[:, bass.ds(t, 1)], rs[p2][:, 1:2]).then_inc(s_ep2, 1)
                link(nc.vector.tensor_scalar(xall[:, t, :], res[p2][:, :], mv[p2][:, 0:1], rs[p2][:, 0:1],
                                             ALU.subtract, ALU.mult))
                dve.wait_ge(s_yst[p2], 16 * c2)
                nc.vector.tensor_scalar(y[p2][:, :], xall[:, t, :], rs[p2][:, 1:2], None, ALU.mult).then_inc(s_y[p2], 1)

            def body(k, b):
                finding, listing = stage(k, b, 1), stage(k, b, 2)
                scattering, summing, norming = stage(k, b, 4), stage(k, b, 5), stage(k, b, 6)
                if live(listing[0]):
                    row_steps(*listing)
                if live(finding[0]):
                    find(*finding)
                if live(listing[0]):
                    entries(*listing)
                if live(scattering[0]):
                    scatter(*scattering)
                if live(summing[0]):
                    residual(*summing)
                if live(norming[0]):
                    norm(*norming)
            iterations(dve, body, LAG)
            nc.vector.scalar_tensor_tensor(out=bad[:, :], in0=most[:, :], scalar=float(P), in1=bad[:, :],
                                           op0=ALU.is_gt, op1=ALU.add).then_inc(s_fin, 1)
            dve.wait_ge(s_flagp, 1)
            nc.vector.tensor_copy(flag[:, :], psS[0:1, 0:1]).then_inc(s_flag, 1)

            dve.wait_ge(s_flag, 1)
            faults = dve.value_load(flag[0:1, 0:1], min_val=0, max_val=1 << 20)
            with dve.If(faults == 0):
                dve.wait_ge(s_yst[0], 16 * (PAIRS + 1))
                dve.wait_ge(s_yst[1], 16 * PAIRS)

                nc.vector.tensor_reduce(jshared[:, :], jall[:, :].rearrange("p (g j q) -> p g q j", j=GROUP,
                                                                            q=CH)[:, :, CH - 1, :],
                                        AX_X, ALU.add).then_inc(s2_prep, 1)
                dve.wait_ge(s2_prep, 1)

                def body2(k, b):
                    t, kk, pp, c2, p2, kg, g2 = stage2(k, b, 0)
                    if live(t):
                        if pp == 0:
                            dve.wait_ge(s2_Gs[g2], 16 * kg)
                            nc.vector.tensor_copy(jixs[g2][:, :], jshared[:, bass.ds(t // GROUP if isinstance(t, int)
                                                                                     else 2 * kg + g2, 1)])
                        dve.wait_ge(s2_G[pp], 16 * (CH - 1) * kk)
                        nc.vector.tensor_copy(jix[pp][:, 0:CH - 1],
                                              jall[:, bass.ds(t * CH, CH - 1)]).then_inc(s2_jix, 1)
                    t, _, _, _, p2 = stage2(k, b, 2)[0:5]
                    r, _, _, _, r2 = stage2(k, b, 5)[0:5]
                    n, _, _, nc2, n2 = stage2(k, b, 6)[0:5]

                    def scatter2(q):
                        if live(t):
                            if q == 0:
                                dve.wait_ge(s2_agg, t - 1 if not isinstance(t, int) else max(t - 1, 0))
                            ins = nc.vector.tensor_scalar(M[p2][:, q, :], iota_e[:, 0:P],
                                                          rall[:, bass.ds(t * CH + q, 1)],
                                                          vall[:, bass.ds(t * CH + q, 1)], ALU.is_equal, ALU.mult)
                            if q == CH - 1:
                                ins.then_inc(s2_M, 1)

                    if live(r):
                        dve.wait_ge(s2_z, r + 1)
                        nc.vector.tensor_scalar(zs[:, :], psZ2[r2][:, 0:D], dinv[:, bass.ds(r, 1)], 0.0,
                                                ALU.mult, ALU.max).then_inc(s2_ep1, 1)
                    scatter2(0)
                    if live(r):
                        dve.wait_ge(s2_ep1, r * 4 + 1)
                        nc.vector.tensor_tensor(res[r2][:, :], xall[:, r, :], zs[:, :], ALU.add).then_inc(s2_ep1, 1)
                    if live(n):
                        dve.wait_ge(s2_std, n + 1)
                        nc.vector.reciprocal(rs[n2][:, 0:1], sq[n2][:, 0:1]).then_inc(s2_n, 1)
                    scatter2(1)
                    if live(r):
                        dve.wait_ge(s2_ep1, r * 4 + 2)
                        nc.vector.bn_stats(stats[:, :], res[r2][:, :]).then_inc(s2_ep1, 1)
                    if live(n):
                        dve.wait_ge(s2_ost[n2], 16 * nc2)
                        dve.wait_ge(s2_n, n + 1)
                        nc.vector.tensor_scalar(y[n2][:, :], res[n2][:, :], mv[n2][:, 0:1], rs[n2][:, 0:1],
                                                ALU.subtract, ALU.mult).then_inc(s2_o[n2], 1)
                    if live(r):
                        dve.wait_ge(s2_ep1, r * 4 + 3)
                        nc.vector.tensor_copy(mv[r2][:, 2:3], stats[:, 0:1])
                        nc.vector.bn_aggr(mv[r2][:, 0:2], stats[:, :]).then_inc(s2_ep1, 1)
                    scatter2(2)
                    if live(r):
                        dve.wait_ge(s2_ep1, r * 4 + 4)
                        nc.vector.tensor_scalar_add(mv[r2][:, 1:2], mv[r2][:, 1:2], EPS).then_inc(s2_var, 1)

                iterations(dve, body2, LAG2, RING2)
            with dve.Else():
                dve.wait_ge(s_yst[0], 16 * (PAIRS + 1))
                dve.wait_ge(s_yst[1], 16 * PAIRS)
                for i in range(2):
                    last = nc.vector.tensor_copy(pick[:, i, :], ident[0:2, i:i + 1].to_broadcast([2, P]))
                last.then_inc(d_sel, 1)
                for b in range(NT):
                    w = widths[b]
                    dve.wait_ge(d_h, b + 1)
                    nc.vector.tensor_copy(feat[0:w, b, 0:D], psZ[0:w, 0:D]).then_inc(d_hc, 1)

                for l in range(2):
                    S = L[l]
                    if l == 1:
                        dve.wait_ge(d_x1st[0], 16 * (PAIRS + 1))
                        dve.wait_ge(d_x1st[1], 16 * PAIRS)

                    def tile(t, k, b, r0):
                        for g in range(1, NG, 2):
                            dve.wait_ge(S["tr"][1], t * HG + g // 2 + 1)
                            dve.wait_ge(S["mm"][1], t * HG + g // 2)
                            nc.vector.tensor_copy(blkT[1], psM[1][:, :]).then_inc(S["cp"][1], 1)
                        step = [t * 5]

                        def chain(ins):
                            ins.then_inc(S["steps"], 1)
                            step[0] = step[0] + 1
                            dve.wait_ge(S["steps"], step[0])

                        if l == 0:
                            dve.wait_ge(S["acc"], t + 1)
                            chain(nc.vector.scalar_tensor_tensor(out=resd, in0=psZ[:, 0:D], scalar=0.0,
                                                                 in1=xin[b], op0=ALU.max, op1=ALU.add))
                        else:
                            dve.wait_ge(S["mm"][1], (t + 1) * HG)
                            chain(nc.vector.tensor_scalar(zs[:, :], psZ[:, 0:D], dinv[:, bass.ds(t, 1)], None, ALU.mult))
                            dve.wait_ge(S["zm"], t + 1)
                            dve.wait_ge(S["xin"][b], 16 * (k + 1))
                            chain(nc.vector.scalar_tensor_tensor(out=resd, in0=psW[:, 0:D], scalar=0.0,
                                                                 in1=xin[b], op0=ALU.max, op1=ALU.add))
                        chain(nc.vector.bn_stats(stats[:, :], resd))
                        if l == 0:
                            nc.vector.tensor_copy(mv[0][:, 2:3], psZ[:, D:C]).then_inc(S["read"], 1)
                        else:
                            nc.vector.tensor_copy(mv[0][:, 2:3], stats[:, 0:1])
                        chain(nc.vector.bn_aggr(mv[0][:, 0:2], stats[:, :]))
                        nc.vector.tensor_scalar_add(mv[0][:, 1:2], mv[0][:, 1:2], EPS).then_inc(S["var"], 1)
                        dve.wait_ge(S["std"], t + 1)
                        chain(nc.vector.reciprocal(rs[0][:, :], sq[0][:, :]))
                        if l == 0:
                            dve.wait_ge(d_x1st[b], 16 * k)
                            dve.wait_ge(d_yst[b], 16 * k)
                            nc.vector.tensor_copy(dinv[:, bass.ds(t, 1)], rs[0][:, 1:2])
                            chain(nc.vector.tensor_scalar(x1d[b], resd, mv[0][:, 0:1], rs[0][:, 0:1],
                                                          ALU.subtract, ALU.mult))
                            nc.vector.tensor_scalar(y[b][:, :], x1d[b], rs[0][:, 1:2], None, ALU.mult
                                                    ).then_inc(S["tile"][b], 1)
                        else:
                            dve.wait_ge(d_ost[b], 16 * k)
                            nc.vector.tensor_scalar(x1d[b], resd, mv[0][:, 0:1], rs[0][:, 0:1],
                                                    ALU.subtract, ALU.mult).then_inc(S["tile"][b], 1)

                    tiles(dve, tile)



_INS = ['x', 'adj', 'L0_gnn_item_feat', 'L0_gnn_W_item', 'L0_gnn_b_item', 'L0_gnn_W_user', 'L0_gnn_b_user', 'L1_gnn_W']
_OUTS = [((10000, 128), 'float32')]


def kernel(**inputs):
    import numpy as _np
    import concourse.bacc as _bacc
    from concourse import mybir as _mybir
    from concourse.bass_utils import run_bass_kernel_spmd as _run

    nc = _bacc.Bacc("TRN2", target_bir_lowering=False, num_devices=1)
    arrays, args = {}, []
    for name in _INS:
        a = _np.ascontiguousarray(inputs[name])
        arrays[f"in_{name}_dram"] = a
        args.append(nc.dram_tensor(f"in_{name}_dram", a.shape, _mybir.dt.from_np(a.dtype), kind="ExternalInput").ap())
    for i, (shape, dtype) in enumerate(_OUTS):
        dt = _mybir.dt.from_np(_np.dtype(dtype))
        args.append(nc.dram_tensor(f"out_{i}_dram", shape, dt, kind="ExternalOutput").ap())
    gnn_kernel(nc, *args)
    r = _run(nc, [arrays], core_ids=[0])
    return r.results[0]["out_0_dram"]
```
